# Optimizing a Trainium2 kernel written in Bass

```python
import numpy as np
import jax
import jax.numpy as jnp

def _softmax(x, axis=-1):
    return jax.nn.softmax(x, axis=axis)

def _gelu(x):
    return jax.nn.gelu(x, approximate=True)

def _silu(x):
    return jax.nn.silu(x)

def _sigmoid(x):
    return jax.nn.sigmoid(x)

def _layernorm(x, axis=-1, eps=1e-05):
    m = jnp.mean(x, axis=axis, keepdims=True)
    v = jnp.var(x, axis=axis, keepdims=True)
    return (x - m) / jnp.sqrt(v + eps)

def _scatter_add(tgt, idx, src, axis=0):
    return tgt.at[idx].add(src)

def _segment_sum(src, seg, n):
    return jax.ops.segment_sum(src, seg, n)
kernel_name = 'mk_vit_tower_cls_d1_tok_img1024_r4_cda388'

def setup_inputs(seed: int=0):
    np.random.seed(seed)
    _w = jnp.asarray

    def _rec_inputs():
        import jax
        import jax.numpy as jnp
        _rk = jax.random.key(seed)
        x = -0.00016672 + 0.999947 * jax.random.normal(jax.random.fold_in(_rk, 1), (32, 3, 96, 96), jnp.float32)
        cls_tok = 0.02 * jax.random.normal(jax.random.fold_in(_rk, 5), (1, 1, 256), jnp.float32)
        return (x, cls_tok)
    x, cls_tok = _rec_inputs()

    def _L0_tok_setup():
        import jax, jax.numpy as jnp
        import numpy as np
        PATCH = 16
        key = jax.random.key(seed)
        k1, k2, k3 = jax.random.split(key, 3)
        B, C, H, Wd = (64, 3, 96, 96)
        patch_dim = C * PATCH * PATCH
        embed_dim = 256
        x = jax.random.normal(k1, (B, C, H, Wd), dtype=jnp.float32)
        W = jax.random.normal(k2, (embed_dim, patch_dim), dtype=jnp.float32) * patch_dim ** (-0.5)
        b = jax.random.normal(k3, (embed_dim,), dtype=jnp.float32) * 0.01
        return {'x': x, 'W': W, 'b': b}
    _L0_tok_all = _L0_tok_setup()
    _L0_tok_in = {k: v for k, v in _L0_tok_all.items() if k in ('W', 'b')}
    del _L0_tok_all

    def _L0_attn_setup():
        import jax, jax.numpy as jnp
        import numpy as np
        B, S, D, H = (4, 512, 256, 4)
        HD = D // H

        def _reference_tuple_inner(hidden_states, Wq, Wk, Wv, Wo, bo, betas, mem, z):
            b, s, d = hidden_states.shape
            h = betas.shape[1]
            hd = d // h

            def split(x):
                return x.reshape(b, s, h, hd).transpose(0, 2, 1, 3)
            q = split(hidden_states @ Wq.T)
            k = split(hidden_states @ Wk.T)
            v = split(hidden_states @ Wv.T)
            aw = jnp.einsum('bhqd,bhkd->bhqk', q, k)
            causal = jnp.tril(jnp.ones((s, s), bool))
            aw = jnp.where(causal, aw, jnp.finfo(aw.dtype).min)
            p = jax.nn.softmax(aw, axis=-1)
            attn = jnp.einsum('bhqk,bhkd->bhqd', p, v)
            sq = jax.nn.elu(q) + 1.0
            sk = jax.nn.elu(k) + 1.0
            A_mem = jnp.einsum('bhsd,hde->bhse', sq, mem) / (jnp.einsum('bhsd,hdo->bhso', sq, z) + 1e-06)
            g = jax.nn.sigmoid(betas)
            out = g * A_mem + (1.0 - g) * attn
            delta = jnp.einsum('bhsd,hde->bhse', sk, mem) / (jnp.einsum('bhsd,hdo->bhso', sk, z) + 1e-06)
            mem_new = mem + jnp.einsum('bhsd,bhse->hde', sk, v - delta) / b
            z_new = z + jnp.mean(jnp.sum(sk, axis=2), axis=0)[:, :, None]
            out = out.transpose(0, 2, 1, 3).reshape(b, s, d)
            out = out @ Wo.T + bo
            return (out, mem_new, z_new)
        key = jax.random.key(seed)
        ks = jax.random.split(key, 6)
        s = 0.02
        return {'hidden_states': jax.random.normal(ks[0], (B, S, D), jnp.float32), 'Wq': jax.random.normal(ks[1], (D, D), jnp.float32) * s, 'Wk': jax.random.normal(ks[2], (D, D), jnp.float32) * s, 'Wv': jax.random.normal(ks[3], (D, D), jnp.float32) * s, 'Wo': jax.random.normal(ks[4], (D, D), jnp.float32) * s, 'bo': jnp.zeros((D,), jnp.float32), 'betas': jax.random.normal(ks[5], (1, H, 1, 1), jnp.float32), 'mem': jnp.zeros((H, HD, HD), jnp.float32), 'z': jnp.zeros((H, HD, 1), jnp.float32)}
    _L0_attn_all = _L0_attn_setup()
    _L0_attn_in = {k: v for k, v in _L0_attn_all.items() if k in ('Wq', 'Wk', 'Wv', 'Wo', 'bo', 'betas', 'mem', 'z')}
    del _L0_attn_all

    def _L0_ffn_setup():
        import jax, jax.numpy as jnp
        import numpy as np
        D_MODEL = 256
        N_EXPERTS = 8
        TOP_K = 2
        HIDDEN = 4 * D_MODEL
        key = jax.random.key(seed)
        ks = jax.random.split(key, 6)
        B, S = (2, 512)
        x = jax.random.normal(ks[0], (B, S, D_MODEL), dtype=jnp.float32)
        shared_w1 = jax.random.normal(ks[1], (HIDDEN, D_MODEL), dtype=jnp.float32) * 0.02
        shared_w2 = jax.random.normal(ks[2], (D_MODEL, HIDDEN), dtype=jnp.float32) * 0.02
        experts_w1 = jax.random.normal(ks[3], (N_EXPERTS, HIDDEN, D_MODEL), dtype=jnp.float32) * 0.02
        experts_w2 = jax.random.normal(ks[4], (N_EXPERTS, D_MODEL, HIDDEN), dtype=jnp.float32) * 0.02
        gate_w = jax.random.normal(ks[5], (N_EXPERTS, D_MODEL), dtype=jnp.float32) * 0.02
        return {'x': x, 'shared_w1': shared_w1, 'shared_w2': shared_w2, 'experts_w1': experts_w1, 'experts_w2': experts_w2, 'gate_w': gate_w}
    _L0_ffn_all = _L0_ffn_setup()
    _L0_ffn_in = {k: v for k, v in _L0_ffn_all.items() if k in ('shared_w1', 'shared_w2', 'experts_w1', 'experts_w2', 'gate_w')}
    del _L0_ffn_all
    return {'x': x, 'cls_tok': cls_tok, 'L0_tok_W': _L0_tok_in['W'], 'L0_tok_b': _L0_tok_in['b'], 'L0_attn_Wq': _L0_attn_in['Wq'], 'L0_attn_Wk': _L0_attn_in['Wk'], 'L0_attn_Wv': _L0_attn_in['Wv'], 'L0_attn_Wo': _L0_attn_in['Wo'], 'L0_attn_bo': _L0_attn_in['bo'], 'L0_attn_betas': _L0_attn_in['betas'], 'L0_attn_mem': _L0_attn_in['mem'], 'L0_attn_z': _L0_attn_in['z'], 'L0_ffn_shared_w1': _L0_ffn_in['shared_w1'], 'L0_ffn_shared_w2': _L0_ffn_in['shared_w2'], 'L0_ffn_experts_w1': _L0_ffn_in['experts_w1'], 'L0_ffn_experts_w2': _L0_ffn_in['experts_w2'], 'L0_ffn_gate_w': _L0_ffn_in['gate_w']}

def reference(x, cls_tok, L0_tok_W, L0_tok_b, L0_attn_Wq, L0_attn_Wk, L0_attn_Wv, L0_attn_Wo, L0_attn_bo, L0_attn_betas, L0_attn_mem, L0_attn_z, L0_ffn_shared_w1, L0_ffn_shared_w2, L0_ffn_experts_w1, L0_ffn_experts_w2, L0_ffn_gate_w):
    import jax
    import jax.numpy as jnp

    def _L0_tok_ref(x, W, b):
        import jax, jax.numpy as jnp
        import numpy as np
        PATCH = 16
        B, C, H, Wd = x.shape
        ph = pw = PATCH
        gh, gw = (H // ph, Wd // pw)
        patches = x.reshape(B, C, gh, ph, gw, pw)
        patches = patches.transpose(0, 2, 4, 1, 3, 5).reshape(B, gh * gw, C * ph * pw)
        out = jnp.einsum('bnp,dp->bnd', patches, W) + b
        return out

    def _L0_attn_ref(hidden_states, Wq, Wk, Wv, Wo, bo, betas, mem, z):
        import jax, jax.numpy as jnp
        import numpy as np
        B, S, D, H = (4, 512, 256, 4)
        HD = D // H

        def _reference_tuple_inner(hidden_states, Wq, Wk, Wv, Wo, bo, betas, mem, z):
            b, s, d = hidden_states.shape
            h = betas.shape[1]
            hd = d // h

            def split(x):
                return x.reshape(b, s, h, hd).transpose(0, 2, 1, 3)
            q = split(hidden_states @ Wq.T)
            k = split(hidden_states @ Wk.T)
            v = split(hidden_states @ Wv.T)
            aw = jnp.einsum('bhqd,bhkd->bhqk', q, k)
            causal = jnp.tril(jnp.ones((s, s), bool))
            aw = jnp.where(causal, aw, jnp.finfo(aw.dtype).min)
            p = jax.nn.softmax(aw, axis=-1)
            attn = jnp.einsum('bhqk,bhkd->bhqd', p, v)
            sq = jax.nn.elu(q) + 1.0
            sk = jax.nn.elu(k) + 1.0
            A_mem = jnp.einsum('bhsd,hde->bhse', sq, mem) / (jnp.einsum('bhsd,hdo->bhso', sq, z) + 1e-06)
            g = jax.nn.sigmoid(betas)
            out = g * A_mem + (1.0 - g) * attn
            delta = jnp.einsum('bhsd,hde->bhse', sk, mem) / (jnp.einsum('bhsd,hdo->bhso', sk, z) + 1e-06)
            mem_new = mem + jnp.einsum('bhsd,bhse->hde', sk, v - delta) / b
            z_new = z + jnp.mean(jnp.sum(sk, axis=2), axis=0)[:, :, None]
            out = out.transpose(0, 2, 1, 3).reshape(b, s, d)
            out = out @ Wo.T + bo
            return (out, mem_new, z_new)
        return _reference_tuple_inner(hidden_states, Wq, Wk, Wv, Wo, bo, betas, mem, z)[0]

    def _L0_ffn_ref(x, shared_w1, shared_w2, experts_w1, experts_w2, gate_w):
        import jax, jax.numpy as jnp
        import numpy as np
        D_MODEL = 256
        N_EXPERTS = 8
        TOP_K = 2
        HIDDEN = 4 * D_MODEL
        B, S, D = x.shape
        T = B * S
        x_flat = x.reshape(T, D)
        shared = jnp.einsum('td,dh->th', x_flat, shared_w1.T)
        shared = jnp.einsum('th,hd->td', jax.nn.silu(shared), shared_w2.T)
        gate_logits = x_flat @ gate_w.T
        top_k_gates, top_k_idx = jax.lax.top_k(gate_logits, TOP_K)
        top_k_gates = jax.nn.softmax(top_k_gates, axis=1)
        gates = jnp.zeros((T, N_EXPERTS), dtype=x.dtype)
        gates = gates.at[jnp.arange(T)[:, None], top_k_idx].set(top_k_gates)
        h = jnp.einsum('td,ehd->teh', x_flat, experts_w1)
        expert_out = jnp.einsum('teh,edh->ted', jax.nn.silu(h), experts_w2)
        selected = jnp.einsum('ted,te->td', expert_out, gates)
        return (shared + selected).reshape(B, S, D)
    h = _L0_tok_ref(x, L0_tok_W, L0_tok_b)
    h = jnp.concatenate([jnp.broadcast_to(cls_tok, (h.shape[0], 1, h.shape[2])), h], axis=1)
    h = h + _L0_attn_ref(_layernorm(h, axis=-1), L0_attn_Wq, L0_attn_Wk, L0_attn_Wv, L0_attn_Wo, L0_attn_bo, L0_attn_betas, L0_attn_mem, L0_attn_z)
    h = h + _L0_ffn_ref(_layernorm(h, axis=-1), L0_ffn_shared_w1, L0_ffn_shared_w2, L0_ffn_experts_w1, L0_ffn_experts_w2, L0_ffn_gate_w)
    return h

_drawn_inputs = setup_inputs


def setup_inputs(seed=0):
    import zlib

    import numpy as np

    out = dict(_drawn_inputs(seed))
    spreads = {'L0_attn_bo': (0.0, 2.0), 'L0_attn_mem': (0.0, 0.1), 'L0_attn_z': (0.0, 0.1)}
    factors = {'cls_tok': 60.097,
     'L0_attn_Wk': 64.0,
     'L0_attn_Wv': 64.0,
     'L0_ffn_shared_w1': 8.0,
     'L0_ffn_shared_w2': 8.0,
     'L0_ffn_experts_w1': 23.279,
     'L0_ffn_experts_w2': 8.0,
     'L0_ffn_gate_w': 22.898}
    for name, (base, spread) in spreads.items():
        noise = np.random.default_rng([zlib.crc32(name.encode()), seed]).standard_normal(out[name].shape)
        drawn = base * np.exp(spread * noise) if base else spread * noise
        out[name] = jnp.asarray(drawn.astype(out[name].dtype))
    for name, factor in factors.items():
        out[name] = (out[name] * factor).astype(out[name].dtype)
    return out
```

```python
from contextlib import ExitStack

import concourse.bass as bass
from concourse import mybir

ALU = mybir.AluOpType
ACT = mybir.ActivationFunctionType
F32 = mybir.dt.float32
F16 = mybir.dt.float16
U32 = mybir.dt.uint32
I32 = mybir.dt.int32
AX_X = mybir.AxisListType.X

P = 128
IMAGES, SEQ, D = 32, 37, 256
PER_TILE = 3
T = PER_TILE * SEQ
NT = -(-IMAGES // PER_TILE)
TOKENS = IMAGES * SEQ
LAST = TOKENS - (NT - 1) * T
HEADS, HD = 4, 64
KC = D // P
PATCH = 768
PC = PATCH // P
EXPERTS, HIDDEN = 8, 1024
HC = HIDDEN // P
SLOT_TILES = (2 * TOKENS + EXPERTS * (P - 1)) // P
ROW = 2 * D + 4
ID_AT, GATE_AT = 2 * D, 2 * D + 2
EPS = 1e-5
X_SCALE, W_SCALE, H_SCALE = 64.0, 64.0, 16.0
CHUNK = 1024
CHUNKS = 4
EW = CHUNKS * 2 * CHUNK
STAGES = 4
EARLY = 5
RING = 5


def build(nc, patches, w_embed, embed_bias, w_qk, w_v, w_o, out_bias, betas, mem, z, w_ffn, w_gate,
          ident, ident16, causal, before, valid, token_id, pad_rows, lower, iota, steps, out):
    slots = nc.dram_tensor("slots", [SLOT_TILES * P, ROW // 2], U32, kind="Internal").ap()

    with ExitStack() as ctx:
        def sb(name, shape, dt=F32):
            return ctx.enter_context(nc.sbuf_tensor(name, shape, dt))

        def sem(name):
            return ctx.enter_context(nc.semaphore(name))

        bank = [ctx.enter_context(nc.psum_tensor(f"bank{i}", [P, 512], F32)) for i in range(8)]

        weights = sb("weights", [P, (EXPERTS + 1) * EW], F16)
        stage = sb("stage", [P, STAGES, CHUNK])
        row_words = sb("row_words", [P, NT, ROW // 2], U32)
        rows = row_words[:].bitcast(F16)
        h2 = sb("h2", [P, NT, D])
        id16 = sb("id16", [P, P], F16)
        gate_pair = sb("gate_pair", [P, KC, 2, EXPERTS], F16)
        top = sb("top", [P, NT, 8])
        top_at = sb("top_at", [P, NT, 8], U32)
        gates = sb("gates", [P, 2, NT])
        gate_gap = sb("gate_gap", [P, 2, NT])
        slot_of = sb("slot_of", [P, 2, NT], U32)
        expert_of = sb("expert_of", [P, SLOT_TILES], I32)

        slot_words = sb("slot_words", [P, 4, ROW // 2], U32)
        slot_rows = slot_words[:].bitcast(F16)
        x_t = sb("x_t", [P, 2, 4 * P], F16)
        act_out = sb("act_out", [P, 2, 512])
        hid_hi = sb("hid_hi", [P, 2, HIDDEN], F16)
        hid_lo = sb("hid_lo", [P, 2, HIDDEN], F16)
        y = sb("y", [P, 3, D])

        space = weights[:, EARLY * EW:].bitcast(F32)
        used = [0]

        def part(*dims):
            n = 1
            for d in dims:
                n *= d
            ap = space[:, used[0]:used[0] + n]
            used[0] += n
            assert used[0] <= (EXPERTS + 1 - EARLY) * EW // 2
            if len(dims) == 2:
                return ap.rearrange("p (a b) -> p a b", b=dims[1])
            if len(dims) == 3:
                return ap.rearrange("p (a b c) -> p a b c", b=dims[1], c=dims[2])
            return ap

        s_we = part(PC, D)
        s_wqk = part(KC, 4, P)
        s_wv = part(KC, D)
        s_wo = part(KC, D)
        s_eb = part(D)
        s_ob = part(D)
        s_id = part(P)
        s_causal = part(T)
        s_beta = part(HEADS)
        s_mem = part(KC, P)
        s_z = part(KC, 2)
        s_wg = part(KC, EXPERTS)
        keep = part(2, HEADS)
        s_patch = part(2, PC, T)
        h = part(RING, D)
        h_bo = part(RING, D)
        xln = part(2, D)
        xln_t = part(2, KC, T)
        qk_t = part(2, 4, T)
        v = part(3, D)
        q_min = part(2, 2, T)
        sq = part(3, 2, T)
        prob = part(2, HEADS * T)
        prob_t = part(2, HEADS * T)
        neg_max = part(2, HEADS)
        row_sum = part(4, HEADS)
        mix = part(2, HEADS)
        read = part(D)
        attn = part(2, D)
        attn_t = part(2, KC, T)
        xln2 = part(2, D)
        x2_t = part(2, 4 * T // 2)
        stats = part(2, 6)
        mv = part(4, 2)
        rstd = part(4)
        newton = part(4)
        var_eps = part(4)
        half = part(1)

        q_den = sb("q_den", [P, 2, T])
        s_before = sb("s_before", [P, T], F16)
        ones = sb("ones", [P, T], F16)
        s_valid = sb("s_valid", [P, NT, 8])
        s_tid = sb("s_tid", [P, NT], U32)
        s_pad = slot_words[:, 3]
        s_lower = sb("s_lower", [P, 8, 8])
        s_iota = sb("s_iota", [P, 8])
        s_steps = sb("s_steps", [P, 10 + SLOT_TILES])
        top_f = sb("top_f", [P, 2, NT])
        temp = y[:].rearrange("p a b -> p (a b)")
        rank = temp[:, 0:96].rearrange("p (a b) -> p a b", b=8)
        pick = temp[:, 96:272].rearrange("p (k a b) -> p k a b", k=2, b=8)
        prod = temp[:, 272:448].rearrange("p (k a b) -> p k a b", k=2, b=8)
        tiles_cmp = temp[:, 448:528].rearrange("p (a b) -> p a b", b=10)
        tri = temp[:, 528:592].rearrange("p (a b) -> p a b", b=8)
        end_cmp = temp[:, 272:272 + 8 * SLOT_TILES].rearrange("p (a b) -> p a b", b=8)
        member = sb("member", [P, NT + 1, 8], F16)
        tiles_of = sb("tiles_of", [P, 3, 8])
        slot_f = sb("slot_f", [P, 2, NT])
        exp_f = sb("exp_f", [P, 2, SLOT_TILES])

        consts_in = sem("consts_in")
        route_in = sem("route_in")
        patches_in = [sem(f"patches_in{i}") for i in range(2)]
        stage_in = [sem(f"stage_in{i}") for i in range(STAGES)]
        pads_out = sem("pads_out")
        dummy_out = sem("dummy_out")

        embed_ready = sem("embed_ready")
        h_ready = sem("h_ready")
        h_bo_ready = sem("h_bo_ready")
        stats1 = sem("stats1")
        rstd1 = sem("rstd1")
        stats2 = sem("stats2")
        rstd2 = sem("rstd2")
        pool_step = sem("pool_step")
        xln_ready = sem("xln_ready")
        xln_turned = sem("xln_turned")
        xln_t_ready = sem("xln_t_ready")
        qk_ready = sem("qk_ready")
        v_ready = sem("v_ready")
        qk_copied = sem("qk_copied")
        v_copied = sem("v_copied")
        q_min_ready = sem("q_min_ready")
        q_tanh_ready = sem("q_tanh_ready")
        sq_ready = sem("sq_ready")
        scores_ready = sem("scores_ready")
        scores_masked = sem("scores_masked")
        max_ready = sem("max_ready")
        prob_ready = sem("prob_ready")
        prob_turned = sem("prob_turned")
        prob_t_ready = sem("prob_t_ready")
        mixed_ready = sem("mixed_ready")
        attn_ready = sem("attn_ready")
        attn_turned = sem("attn_turned")
        attn_t_ready = sem("attn_t_ready")
        wo_ready = sem("wo_ready")
        h2_ready = sem("h2_ready")
        xln2_ready = sem("xln2_ready")
        row_hi_ready = sem("row_hi_ready")
        row_lo_ready = sem("row_lo_ready")
        x2_turned = sem("x2_turned")
        x2_t_ready = sem("x2_t_ready")
        logits_ready = sem("logits_ready")
        gap_ready = sem("gap_ready")
        gap_exp = sem("gap_exp")
        top_done = sem("top_done")
        beta_exp = sem("beta_exp")
        gate_hi = sem("gate_hi")
        gate_pair_ready = sem("gate_pair_ready")
        ones_ready = sem("ones_ready")
        dve_step = sem("dve_step")
        members_ready = sem("members_ready")
        ranks_ready = sem("ranks_ready")
        slots_known = sem("slots_known")
        second_gates = sem("second_gates")
        experts_known = sem("experts_known")
        scattered = [sem("scattered1"), sem("scattered2")]
        w_scaled = sem("w_scaled")
        w_hi = sem("w_hi")
        w_lo = sem("w_lo")
        w_lo_late = sem("w_lo_late")

        slot_rows_in = [sem(f"slot_rows_in{i}") for i in range(4)]
        x_turned = sem("x_turned")
        x_t_ready = sem("x_t_ready")
        hid_ready = sem("hid_ready")
        hid_acted = sem("hid_acted")
        hi_ready = sem("hi_ready")
        lo_ready = sem("lo_ready")
        y_ready = sem("y_ready")
        y_scaled = sem("y_scaled")
        shared_out = [sem(f"shared_out{i}") for i in range(3)]
        added = sem("added")

        def staged(eng, c):
            eng.wait_ge(stage_in[c % STAGES], 16 * (c // STAGES + 1))

        NCHUNK = (EXPERTS + 1) * CHUNKS
        FRONT_CHUNKS = EARLY * CHUNKS
        STEPS = NT + 5
        LOOP_CHUNKS = NCHUNK - FRONT_CHUNKS

        def chunks_at(step):
            return range(FRONT_CHUNKS * step // STEPS, FRONT_CHUNKS * (step + 1) // STEPS)

        def hi_of(c):
            return weights[:, bass.ds(2 * CHUNK * c, CHUNK)]

        def lo_of(c):
            return weights[:, bass.ds(2 * CHUNK * c + CHUNK, CHUNK)]

        def w_rows(c):
            return w_ffn[c // CHUNKS, :, CHUNK * (c % CHUNKS):CHUNK * (c % CHUNKS + 1)]

        block = ctx.enter_context(nc.Block())

        S0 = NT

        @block.sync
        def _(sp):
            def load_chunk(c):
                last = c - STAGES
                if last >= FRONT_CHUNKS:
                    sp.wait_ge(w_lo_late, last - FRONT_CHUNKS + 1)
                elif last >= 0:
                    sp.wait_ge(w_lo, last + 1)
                sp.dma_start(stage[:, c % STAGES], w_rows(c)).then_inc(stage_in[c % STAGES], 16)

            def load_patches(t):
                if t >= 2:
                    sp.wait_ge(embed_ready, t - 1)
                sp.dma_start(s_patch[:, t % 2].rearrange("p a b -> p (a b)"),
                             patches[t]).then_inc(patches_in[t % 2], 16)

            load_patches(0)
            sp.dma_start(s_we.rearrange("p a b -> p (a b)"), w_embed).then_inc(consts_in, 16)
            for dst, src in ((s_eb[0:T], embed_bias), (s_id, ident), (s_ob[0:T], out_bias),
                             (s_wqk.rearrange("p a b c -> p (a b c)"), w_qk),
                             (s_wv.rearrange("p a b -> p (a b)"), w_v),
                             (s_wo.rearrange("p a b -> p (a b)"), w_o),
                             (s_causal[0:T], causal), (s_beta[0:T], betas),
                             (s_mem.rearrange("p a b -> p (a b)"), mem),
                             (s_z.rearrange("p a b -> p (a b)"), z),
                             (s_wg.rearrange("p a b -> p (a b)"), w_gate),
                             (id16[:], ident16)):
                sp.dma_start(dst, src).then_inc(consts_in, 16)
            load_patches(1)
            for dst, src in ((s_before[0:T], before), (s_valid[0:T], valid), (s_tid[0:T], token_id),
                             (s_pad, pad_rows), (s_lower[0:T], lower), (s_iota[0:T], iota),
                             (s_steps[0:T], steps)):
                sp.dma_start(dst, src).then_inc(route_in, 16)
            load_chunk(0)
            load_chunk(1)
            sp.wait_ge(route_in, 7 * 16)
            for j in range(SLOT_TILES):
                sp.dma_start(slots[j * P:(j + 1) * P], s_pad).then_inc(pads_out, 16)
            sp.dma_start(out[TOKENS:TOKENS + P], s_pad[:, 0:D].bitcast(F32)).then_inc(dummy_out, 16)
            loaded = 2
            for step in range(STEPS):
                if step + 2 < NT:
                    load_patches(step + 2)
                while loaded < min(chunks_at(step).stop + 2, FRONT_CHUNKS):
                    load_chunk(loaded)
                    loaded += 1
            for c in range(FRONT_CHUNKS, NCHUNK):
                load_chunk(c)

            sp.wait_ge(scattered[1], 16 * NT)
            sp.wait_ge(pads_out, 16 * SLOT_TILES)

            def load_slots(j, b):
                sp.dma_start(slot_words[:, b], slots[bass.ds(j * P, P)]).then_inc(slot_rows_in[b], 16)

            for j in range(4):
                load_slots(j, j)
            with sp.Fori(1, (SLOT_TILES - 4) // 4 + 1) as i:
                for b in range(4):
                    sp.wait_ge(added, 16 * (4 * i + b - 3))
                    load_slots(4 * i + b, b)
            for j in range(SLOT_TILES // 4 * 4, SLOT_TILES):
                sp.wait_ge(added, 16 * (j - 3))
                load_slots(j, j % 4)

        @block.tensor
        def _(pe):
            def scores(t):
                pe.wait_ge(qk_copied, t + 1)
                if t >= 1:
                    pe.wait_ge(scores_masked, t)
                if t >= 2:
                    pe.wait_ge(attn_ready, t - 1)
                if t >= 4:
                    pe.wait_ge(top_done, t - 3)
                for hd in range(HEADS):
                    at = slice(HD * (hd % 2), HD * (hd % 2) + HD)
                    to = bank[7 * (hd % 2)][0:T, (hd // 2) * T:(hd // 2 + 1) * T]
                    mm = nc.tensor.matmul(to, qk_t[at, t % 2, hd // 2],
                                          qk_t[at, t % 2, 2 + hd // 2], start=True, stop=True)
                mm.then_inc(scores_ready, 1)

            def turn_prob(t):
                pe.wait_ge(prob_ready, t + 1)
                if t >= 1:
                    pe.wait_ge(prob_t_ready, t)
                for hd in range(HEADS):
                    mm = nc.tensor.transpose(bank[2][0:T, hd * T:(hd + 1) * T],
                                             prob[0:T, t % 2, hd * T:(hd + 1) * T], s_id[0:T, 0:T])
                mm.then_inc(prob_turned, 1)

            def turn_attn(t):
                pe.wait_ge(attn_ready, t + 1)
                if t >= 1:
                    pe.wait_ge(attn_t_ready, t)
                if t >= 2:
                    pe.wait_ge(x2_t_ready, t - 1)
                for k in range(KC):
                    mm = nc.tensor.transpose(bank[3][:, k * T:(k + 1) * T],
                                             attn[0:T, t % 2, k * P:(k + 1) * P], s_id[0:T, 0:T])
                mm.then_inc(attn_turned, 1)

            def turn_xln(t):
                pe.wait_ge(xln_ready, t + 1)
                if t >= 1:
                    pe.wait_ge(xln_t_ready, t)
                if t >= 3:
                    pe.wait_ge(attn_ready, t - 2)
                for k in range(KC):
                    mm = nc.tensor.transpose(bank[1][:, k * T:(k + 1) * T],
                                             xln[0:T, t % 2, k * P:(k + 1) * P], s_id[0:T, 0:T])
                mm.then_inc(xln_turned, 1)

            def embed(t):
                if t == 0:
                    pe.wait_ge(consts_in, 13 * 16)
                pe.wait_ge(patches_in[t % 2], 16 * (t // 2 + 1))
                if t >= 5:
                    pe.wait_ge(h2_ready, t - 4)
                if t >= 1:
                    pe.wait_ge(h_ready, t)
                for k in range(PC):
                    mm = nc.tensor.matmul(bank[4][0:T, 0:D], s_patch[:, t % 2, k], s_we[:, k],
                                          start=(k == 0), stop=(k == PC - 1))
                mm.then_inc(embed_ready, 1)

            def turn_rows(t):
                pe.wait_ge(row_lo_ready, t + 1)
                pe.wait_ge(attn_t_ready, min(t + 2, NT))
                if t >= 1:
                    pe.wait_ge(x2_t_ready, t)
                for q in range(4):
                    mm = nc.tensor.transpose(bank[3][:].bitcast(F16)[:, q * 128:q * 128 + T],
                                             rows[0:T, t, q * P:(q + 1) * P], id16[0:T, 0:T])
                mm.then_inc(x2_turned, 1)

            def project(t):
                pe.wait_ge(xln_t_ready, t + 1)
                if t >= 1:
                    pe.wait_ge(qk_copied, t)
                for o in range(4):
                    for k in range(KC):
                        mm = nc.tensor.matmul(bank[5][:, o * T:(o + 1) * T], s_wqk[:, k, o],
                                              xln_t[:, t % 2, k], start=(k == 0), stop=(k == KC - 1))
                mm.then_inc(qk_ready, 1)
                if t >= 1:
                    pe.wait_ge(v_copied, t)
                for k in range(KC):
                    mm = nc.tensor.matmul(bank[6][0:T, 0:D], xln_t[:, t % 2, k], s_wv[:, k],
                                          start=(k == 0), stop=(k == KC - 1))
                mm.then_inc(v_ready, 1)

            def mix_values(t):
                pe.wait_ge(prob_t_ready, t + 1)
                pe.wait_ge(v_copied, t + 1)
                pe.wait_ge(sq_ready, t + 1)
                pe.wait_ge(scores_masked, min(t + 2, NT))
                for hd in range(HEADS):
                    nc.tensor.matmul(bank[7][0:T, hd * HD:(hd + 1) * HD],
                                     prob_t[0:T, t % 2, hd * T:(hd + 1) * T],
                                     v[0:T, t % 3, hd * HD:(hd + 1) * HD], start=True, stop=True)
                for k in range(KC):
                    nc.tensor.matmul(bank[7][0:T, D + k * P:D + (k + 1) * P], sq[:, t % 3, k],
                                     s_mem[:, k], start=True, stop=True)
                pe.wait_ge(xln_t_ready, min(t + 3, NT))
                for k in range(KC):
                    mm = nc.tensor.matmul(bank[1][0:T, 2 * k:2 * k + 2], sq[:, t % 3, k],
                                          s_z[:, k], start=True, stop=True)
                mm.then_inc(mixed_ready, 1)

            def project_out(t):
                pe.wait_ge(attn_t_ready, t + 1)
                pe.wait_ge(h_ready, min(t + 5, NT))
                if t >= 1:
                    pe.wait_ge(h2_ready, t)
                for k in range(KC):
                    mm = nc.tensor.matmul(bank[4][0:T, D:2 * D], attn_t[:, t % 2, k], s_wo[:, k],
                                          start=(k == 0), stop=(k == KC - 1))
                mm.then_inc(wo_ready, 1)

            def logits(t):
                pe.wait_ge(x2_t_ready, t + 1)
                if t == 0:
                    pe.wait_ge(gate_pair_ready, 1)
                pe.wait_ge(attn_ready, min(t + 3, NT))
                if t >= 1:
                    pe.wait_ge(top_done, t)
                turned = x2_t[:, t % 2].bitcast(F16)
                prods = [(0, 0), (0, 1), (1, 0)]
                for k in range(KC):
                    for n, (a, b) in enumerate(prods):
                        q = 2 * a + k
                        mm = nc.tensor.matmul(bank[7][0:T, 0:EXPERTS], turned[:, q * T:(q + 1) * T],
                                              gate_pair[:, k, b], start=(k == 0 and n == 0),
                                              stop=(k == KC - 1 and n == 2))
                mm.then_inc(logits_ready, 1)

            for s in range(STEPS):
                if 0 <= s - 3 < NT:
                    turn_prob(s - 3)
                if 0 <= s - 4 < NT:
                    turn_attn(s - 4)
                if 0 <= s - 1 < NT:
                    turn_xln(s - 1)
                if s < NT:
                    embed(s)
                if 0 <= s - 2 < NT:
                    scores(s - 2)
                if 0 <= s - 5 < NT:
                    turn_rows(s - 5)
                if 0 <= s - 1 < NT:
                    project(s - 1)
                if 0 <= s - 3 < NT:
                    mix_values(s - 3)
                if 0 <= s - 4 < NT:
                    project_out(s - 4)
                if 0 <= s - 5 < NT:
                    logits(s - 5)

            def ranks():
                pe.wait_ge(members_ready, 1)
                pe.wait_ge(route_in, 7 * 16)
                pe.wait_ge(ones_ready, 1)
                flat = bank[7][0:T, 0:(NT + 1) * 8]
                nc.tensor.matmul(flat, s_before[0:T, :], member[0:T].rearrange("p a b -> p (a b)"),
                                 start=True, stop=False)
                for t in range(NT):
                    later = flat[:, (t + 1) * 8:].rearrange("p (a b) -> p a b", b=8)
                    src = member[0:T, t:t + 1, :].broadcast_to([T, NT - t, 8])
                    mm = nc.tensor.matmul(later, ones[0:T, :], src, start=False, stop=(t == NT - 1))
                mm.then_inc(ranks_ready, 1)

            def turn(n, b, src, m):
                pe.wait_ge(x_t_ready, n)
                for q in range(4):
                    mm = nc.tensor.transpose(bank[4][:].bitcast(F16)[:, q * P:q * P + m],
                                             src[0:m, q * P:(q + 1) * P], id16[0:m, 0:m])
                mm.then_inc(x_turned, 1)

            def up(n, b, m, base, first=False):
                pe.wait_ge(x_t_ready, n + 1)
                for half_ in range(2):
                    if not first:
                        pe.wait_ge(hid_acted, 2 * n - 3 + half_)
                    for c in range(4):
                        o = bank[2 * b + half_][:, c * P:c * P + m]
                        col = (4 * half_ + c) * P
                        for k in range(KC):
                            for w, x in ((0, 0), (0, 1), (1, 0)):
                                mm = nc.tensor.matmul(
                                    o, weights[:, bass.ds(base + (2 * k + w) * CHUNK + col, P)],
                                    x_t[:, b, (2 * x + k) * P:(2 * x + k) * P + m],
                                    start=(k == 0 and w + x == 0), stop=(k == 1 and w == 1))
                    mm.then_inc(hid_ready, 1)

            def down(n, b, m, base, first=False):
                if not first:
                    pe.wait_ge(y_scaled, n - 1)
                for c in range(HC):
                    if c % 4 == 0:
                        pe.wait_ge(lo_ready, 2 * n + c // 4 + 1)
                    for hid, w in ((hid_hi, 0), (hid_hi, 1), (hid_lo, 0)):
                        mm = nc.tensor.matmul(
                            bank[5 + b][0:m, 0:D], hid[:, b, c * P:c * P + m],
                            weights[:, bass.ds(base + (4 + 2 * (c // 4) + w) * CHUNK + (c % 4) * D, D)],
                            start=(c == 0 and hid is hid_hi and w == 0),
                            stop=(c == HC - 1 and hid is hid_lo))
                mm.then_inc(y_ready, 1)

            pe.wait_ge(h2_ready, NT)
            turn(0, 0, rows[:, 0], T)
            pe.wait_ge(attn_ready, NT)
            pe.wait_ge(x2_t_ready, NT)
            pe.wait_ge(w_lo, CHUNKS)
            up(0, 0, T, 0, first=True)
            ranks()
            turn(1, 1, rows[:, 1], T)
            up(1, 1, T, 0, first=True)
            turn(2, 0, rows[:, 2], T)
            down(0, 0, T, 0, first=True)
            with pe.Fori(1, (NT - 1) // 2) as i:
                n = 2 * i
                for b in range(2):
                    up(n + b, b, T, 0)
                    turn(n + b + 1, 1 - b, rows[:, bass.ds(n + b + 1, 1)].rearrange("p a b -> p (a b)"), T)
                    if b == 0:
                        down(n - 1, 1, T, 0)
                    else:
                        down(n, 0, T, 0)
            up(NT - 1, 0, T, 0)
            down(NT - 2, 1, T, 0)

            def expert(j):
                return pe.value_load(expert_of[0:1, bass.ds(j, 1)], min_val=EW, max_val=EXPERTS * EW)

            def rows_of(j, r, quad):
                pe.wait_ge(slot_rows_in[r], 16 * (quad + 1))
                turn(NT + j, (NT + r) % 2, slot_rows[:, r], P)

            rows_of(0, 0, 0)
            down(NT - 1, 0, T, 0)
            pe.wait_ge(experts_known, 1)
            pe.wait_ge(w_lo, FRONT_CHUNKS)
            pe.wait_ge(w_lo_late, LOOP_CHUNKS)
            up(NT, NT % 2, P, expert(0))
            rows_of(1, 1, 0)

            def slot_step(j, r, quad_next):
                up(NT + j, (NT + r) % 2, P, expert(j))
                if quad_next is not None:
                    rows_of(j + 1, (r + 1) % 4, quad_next)
                down(NT + j - 1, (NT + r + 1) % 2, P, expert(j - 1))

            SLOT_LOOP = (SLOT_TILES - 2) // 4
            with pe.Fori(0, SLOT_LOOP) as i:
                for r in range(1, 5):
                    slot_step(4 * i + r, r % 4, i + (r + 1) // 4)
            for j in range(4 * SLOT_LOOP + 1, SLOT_TILES):
                slot_step(j, j % 4, (j + 1) // 4 if j + 1 < SLOT_TILES else None)
            down(NT + SLOT_TILES - 1, (NT + SLOT_TILES - 1) % 2, P, expert(SLOT_TILES - 1))

        @block.scalar
        def _(act):
            def exps(t):
                act.wait_ge(max_ready, t + 1)
                for hd in range(HEADS):
                    at = slice(hd * T, (hd + 1) * T)
                    last = nc.scalar.activation(prob[0:T, t % 2, at], prob[0:T, t % 2, at], ACT.Exp,
                                                bias=neg_max[0:T, t % 2, hd:hd + 1],
                                                accum_out=row_sum[0:T, t % 4, hd:hd + 1])
                last.then_inc(prob_ready, 1)

            def copy_xln_t(t):
                act.wait_ge(xln_turned, t + 1)
                if t >= 2:
                    act.wait_ge(v_ready, t - 1)
                nc.scalar.copy(xln_t[:, t % 2].rearrange("p a b -> p (a b)"),
                               bank[1][:, 0:KC * T]).then_inc(xln_t_ready, 1)

            def copy_prob_t(t):
                act.wait_ge(prob_turned, t + 1)
                if t >= 2:
                    act.wait_ge(mixed_ready, t - 1)
                nc.scalar.copy(prob_t[0:T, t % 2], bank[2][0:T, 0:HEADS * T]).then_inc(prob_t_ready, 1)

            def copy_attn_t(t):
                act.wait_ge(attn_turned, t + 1)
                if t >= 2:
                    act.wait_ge(wo_ready, t - 1)
                nc.scalar.copy(attn_t[:, t % 2].rearrange("p a b -> p (a b)"),
                               bank[3][:, 0:KC * T]).then_inc(attn_t_ready, 1)

            def copy_x2_t(t):
                act.wait_ge(x2_turned, t + 1)
                if t >= 2:
                    act.wait_ge(logits_ready, t - 1)
                nc.scalar.copy(x2_t[:, t % 2].bitcast(F16).rearrange("p (a b) -> p a b", b=T),
                               bank[3][:].bitcast(F16)[:, 0:512].rearrange("p (a b) -> p a b", b=128)[:, :, 0:T]
                               ).then_inc(x2_t_ready, 1)

            def copy_qkv(t):
                act.wait_ge(qk_ready, t + 1)
                if t >= 2:
                    act.wait_ge(scores_ready, t - 1)
                nc.scalar.copy(qk_t[:, t % 2].rearrange("p a b -> p (a b)"),
                               bank[5][:, 0:4 * T]).then_inc(qk_copied, 1)
                act.wait_ge(v_ready, t + 1)
                if t >= 3:
                    act.wait_ge(mixed_ready, t - 2)
                nc.scalar.copy(v[0:T, t % 3], bank[6][0:T, 0:D]).then_inc(v_copied, 1)

            def tanh_q(t):
                act.wait_ge(q_min_ready, t + 1)
                nc.scalar.activation(q_min[:, t % 2].rearrange("p a b -> p (a b)"),
                                     q_min[:, t % 2].rearrange("p a b -> p (a b)"),
                                     ACT.Tanh, scale=0.5).then_inc(q_tanh_ready, 1)

            def split_hi(c):
                act.wait_ge(w_scaled, c + 1)
                nc.scalar.copy(hi_of(c), stage[:, c % STAGES]).then_inc(w_hi, 1)

            def row_hi(t):
                act.wait_ge(xln2_ready, t + 1)
                nc.scalar.mul(rows[0:T, t, 0:D], xln2[0:T, t % 2], X_SCALE).then_inc(row_hi_ready, 1)

            def exp_gap(t):
                act.wait_ge(gap_ready, t + 1)
                nc.scalar.activation(gate_gap[0:T, 1, t:t + 1], gate_gap[0:T, 0, t:t + 1],
                                     ACT.Exp).then_inc(gap_exp, 1)

            act.wait_ge(consts_in, 13 * 16)
            nc.scalar.activation(keep[0:T, 1], s_beta[0:T], ACT.Exp, scale=-1.0).then_inc(beta_exp, 1)
            nc.scalar.mul(gate_pair[:, :, 0], s_wg, W_SCALE).then_inc(gate_hi, 1)
            for s in range(STEPS):
                if 0 <= s - 3 < NT:
                    copy_prob_t(s - 3)
                if 0 <= s - 4 < NT:
                    copy_attn_t(s - 4)
                if 0 <= s - 1 < NT:
                    copy_xln_t(s - 1)
                if 0 <= s - 5 < NT:
                    copy_x2_t(s - 5)
                if 0 <= s - 2 < NT:
                    exps(s - 2)
                if 0 <= s - 1 < NT:
                    copy_qkv(s - 1)
                    tanh_q(s - 1)
                for c in chunks_at(s):
                    split_hi(c)
                if 0 <= s - 4 < NT:
                    row_hi(s - 4)
                if 0 <= s - 5 < NT:
                    exp_gap(s - 5)

            def copy_x_t(n, b, m, first=False):
                act.wait_ge(x_turned, n + 1)
                if not first:
                    act.wait_ge(hid_ready, 2 * n - 2)
                v_ = bank[4][:].bitcast(F16)[:, 0:4 * P].rearrange("p (a b) -> p a b", b=P)
                d_ = x_t[:, b].rearrange("p (a b) -> p a b", b=P)
                nc.scalar.copy(d_[:, :, 0:m], v_[:, :, 0:m]).then_inc(x_t_ready, 1)

            def silu(n, b, m, first=False):
                for half_ in range(2):
                    act.wait_ge(hid_ready, 2 * n + half_ + 1)
                    if not first:
                        act.wait_ge(lo_ready, 2 * n + half_ - 1)
                    d_ = act_out[:, half_].rearrange("p (a b) -> p a b", b=P)[:, :, 0:m]
                    s_ = bank[2 * b + half_][:].rearrange("p (a b) -> p a b", b=P)[:, :, 0:m]
                    nc.scalar.activation(d_, s_, ACT.Silu,
                                         scale=1.0 / (X_SCALE * W_SCALE)).then_inc(hid_acted, 1)

            copy_x_t(0, 0, T, first=True)
            silu(0, 0, T, first=True)
            copy_x_t(1, 1, T, first=True)
            silu(1, 1, T)
            copy_x_t(2, 0, T)
            act.wait_ge(wo_ready, NT)
            act.wait_ge(logits_ready, NT)
            act.wait_ge(row_lo_ready, NT)
            PER_TURN = LOOP_CHUNKS // ((NT - 3) // 2)
            with act.Fori(0, (NT - 3) // 2) as i:
                n = 2 * i + 2
                for b in range(2):
                    silu(n + b, b, T)
                    copy_x_t(n + b + 1, 1 - b, T)
                    for c in range(PER_TURN // 2):
                        at = b * (PER_TURN // 2) + c
                        act.wait_ge(stage_in[(FRONT_CHUNKS + at) % STAGES],
                                    16 * (i * (PER_TURN // STAGES) + (FRONT_CHUNKS + at) // STAGES + 1))
                        nc.scalar.mul(hi_of(PER_TURN * i + FRONT_CHUNKS + at),
                                      stage[:, (FRONT_CHUNKS + at) % STAGES], W_SCALE).then_inc(w_hi, 1)
            silu(NT - 1, 0, T)
            copy_x_t(NT, 1, P)
            with act.Fori(0, (SLOT_TILES - 2) // 2) as i:
                for r in range(2):
                    n = 2 * i + r + NT
                    silu(n, (NT + r) % 2, P)
                    copy_x_t(n + 1, (NT + r + 1) % 2, P)
            n = NT + (SLOT_TILES - 2) // 2 * 2
            for n in range(n, NT + SLOT_TILES):
                silu(n, n % 2, P)
                if n + 1 < NT + SLOT_TILES:
                    copy_x_t(n + 1, (n + 1) % 2, P)

        @block.gpsimd
        def _(pool):
            steps_done = [0]

            def link(ins):
                steps_done[0] += 1
                ins.then_inc(pool_step, 1)
                pool.wait_ge(pool_step, steps_done[0])

            def inv_std(t, src, done, slot):
                pool.wait_ge(src, t + 1)
                link(nc.gpsimd.tensor_scalar_add(var_eps[0:T, slot:slot + 1], mv[0:T, slot, 1:2], EPS))
                v_, y_ = var_eps[0:T, slot:slot + 1], rstd[0:T, slot:slot + 1]
                t_ = newton[0:T, slot:slot + 1]
                link(nc.gpsimd.tensor_tensor(y_, v_, half[0:T, 0:1], ALU.pow))
                link(nc.gpsimd.tensor_tensor(t_, y_, y_, ALU.mult))
                link(nc.gpsimd.tensor_tensor(t_, t_, v_, ALU.mult))
                link(nc.gpsimd.tensor_scalar(t_, t_, -0.5, 1.5, ALU.mult, ALU.add))
                nc.gpsimd.tensor_tensor(y_, y_, t_, ALU.mult).then_inc(done, 1)

            def scale_weights(c):
                staged(pool, c)
                nc.gpsimd.tensor_scalar(stage[:, c % STAGES], stage[:, c % STAGES], W_SCALE, 1.0,
                                        ALU.mult, ALU.mult).then_inc(w_scaled, 1)

            def split_lo(c):
                pool.wait_ge(w_hi, c + 1)
                nc.gpsimd.tensor_tensor(lo_of(c), stage[:, c % STAGES], hi_of(c),
                                        ALU.subtract).then_inc(w_lo, 1)

            link(nc.gpsimd.memset(half[:], -0.5))
            nc.gpsimd.memset(ones[:], 1.0).then_inc(ones_ready, 1)
            pool.wait_ge(consts_in, 13 * 16)
            for s in range(STEPS):
                if s < NT:
                    inv_std(s, stats1, rstd1, s % 2)
                    pool.wait_ge(h_ready, s + 1)
                    if s >= RING:
                        pool.wait_ge(h2_ready, s - RING + 1)
                    nc.gpsimd.tensor_tensor(h_bo[0:T, s % RING], h[0:T, s % RING], s_ob[0:T],
                                            ALU.add).then_inc(h_bo_ready, 1)
                if 0 <= s - 4 < NT:
                    inv_std(s - 4, stats2, rstd2, 2 + s % 2)
                for c in chunks_at(s):
                    scale_weights(c)
                for c in chunks_at(s):
                    split_lo(c)

            pool.wait_ge(row_lo_ready, NT)
            pool.wait_ge(pads_out, 16 * SLOT_TILES)
            for k in range(2):
                pool.wait_ge(second_gates if k else slots_known, 1)
                for t in range(NT):
                    m = T if t < NT - 1 else LAST
                    nc.gpsimd.indirect_dma_start(
                        out=slots, out_offset=bass.IndirectOffsetOnAxis(ap=slot_of[0:m, k, t:t + 1], axis=0),
                        in_=row_words[0:m, t, :], in_offset=None).then_inc(scattered[k], 16)

            for t in range(NT):
                m = T if t < NT - 1 else LAST
                pool.wait_ge(y_scaled, t + 1)
                pool.dma_start(out[t * T:t * T + m], y[0:m, t % 3]).then_inc(shared_out[t % 3], 16)
            for q in range(3):
                pool.wait_ge(shared_out[q], 16 * len(range(q, NT, 3)))
            pool.wait_ge(dummy_out, 16)
            for j in range(SLOT_TILES):
                pool.wait_ge(y_scaled, NT + j + 1)
                if j:
                    pool.wait_ge(added, 16 * j)
                nc.gpsimd.indirect_dma_start(
                    out=out, out_offset=bass.IndirectOffsetOnAxis(
                        ap=slot_rows[:, j % 4, ID_AT:ID_AT + 2].bitcast(U32), axis=0),
                    in_=y[:, (NT + j) % 2], in_offset=None, compute_op=ALU.add).then_inc(added, 16)
            pool.wait_ge(added, 16 * SLOT_TILES)

        @block.vector
        def _(dve):
            steps_done = [0]

            def link(ins):
                steps_done[0] += 1
                ins.then_inc(dve_step, 1)
                dve.wait_ge(dve_step, steps_done[0])

            def mask_and_max(t):
                dve.wait_ge(scores_ready, t + 1)
                if t >= 2:
                    dve.wait_ge(prob_turned, t - 1)
                by_pair = prob[0:T, t % 2].rearrange("p (a b c) -> p a b c", b=2, c=T)
                mask = s_causal[0:T].rearrange("p (a b) -> p a b", a=1).broadcast_to([T, 2, T])
                nc.vector.tensor_tensor(
                    by_pair[:, :, 0], bank[0][0:T, 0:2 * T].rearrange("p (a b) -> p a b", b=T), mask, ALU.add)
                nc.vector.tensor_tensor(
                    by_pair[:, :, 1], bank[7][0:T, 0:2 * T].rearrange("p (a b) -> p a b", b=T), mask,
                    ALU.add).then_inc(scores_masked, 1)
                dve.wait_ge(scores_masked, t + 1)
                nc.vector.tensor_reduce(neg_max[0:T, t % 2], prob[0:T, t % 2].rearrange(
                    "p (a b) -> p a b", b=T), AX_X, ALU.max, negate=True).then_inc(max_ready, 1)

            def layer_stats(src, slot, done):
                link(nc.vector.bn_stats(stats[0:T, slot // 2], src))
                nc.vector.bn_aggr(mv[0:T, slot], stats[0:T, slot // 2]).then_inc(done, 1)

            def embed_h(t):
                dve.wait_ge(embed_ready, t + 1)
                nc.vector.tensor_tensor(h[0:T, t % RING], bank[4][0:T, 0:D], s_eb[0:T],
                                        ALU.add).then_inc(h_ready, 1)
                dve.wait_ge(h_ready, t + 1)
                layer_stats(h[0:T, t % RING], t % 2, stats1)

            def norm1(t):
                dve.wait_ge(rstd1, t + 1)
                if t >= 2:
                    dve.wait_ge(xln_turned, t - 1)
                nc.vector.tensor_scalar(xln[0:T, t % 2], h[0:T, t % RING], mv[0:T, t % 2, 0:1],
                                        rstd[0:T, t % 2:t % 2 + 1], ALU.subtract,
                                        ALU.mult).then_inc(xln_ready, 1)

            def min_q(t):
                dve.wait_ge(qk_copied, t + 1)
                nc.vector.tensor_scalar(q_min[:, t % 2], qk_t[:, t % 2, 0:2], 0.0, None,
                                        ALU.min).then_inc(q_min_ready, 1)

            def finish_sq(t):
                dve.wait_ge(q_tanh_ready, t + 1)
                th = q_min[:, t % 2]
                link(nc.vector.tensor_scalar(q_den[:], th, -1.0, 1.0, ALU.mult, ALU.add))
                link(nc.vector.reciprocal(q_den[:], q_den[:]))
                link(nc.vector.scalar_tensor_tensor(out=q_den[:], in0=th, scalar=1.0, in1=q_den[:],
                                                    op0=ALU.add, op1=ALU.mult))
                if t >= 3:
                    dve.wait_ge(mixed_ready, t - 2)
                nc.vector.scalar_tensor_tensor(out=sq[:, t % 3], in0=qk_t[:, t % 2, 0:2], scalar=0.0,
                                               in1=q_den[:], op0=ALU.max,
                                               op1=ALU.add).then_inc(sq_ready, 1)

            def heads(ap):
                return ap.rearrange("p (a b) -> p a b", b=HD)

            def per_head(ap):
                return ap.rearrange("p (a b) -> p a b", b=1).broadcast_to([T, HEADS, HD])

            def combine(t):
                dve.wait_ge(prob_ready, t + 1)
                dve.wait_ge(mixed_ready, t + 1)
                link(nc.vector.tensor_scalar(mix[0:T, 0, 0:HEADS], bank[1][0:T, 0:HEADS], 1e-6, None,
                                             ALU.add))
                link(nc.vector.reciprocal(mix[0:T, 0], mix[0:T, 0]))
                link(nc.vector.tensor_tensor(mix[0:T, 0], mix[0:T, 0], keep[0:T, 0], ALU.mult))
                link(nc.vector.reciprocal(mix[0:T, 1], row_sum[0:T, t % 4]))
                link(nc.vector.tensor_tensor(mix[0:T, 1], mix[0:T, 1], keep[0:T, 1], ALU.mult))
                nc.vector.tensor_tensor(heads(read[0:T]), heads(bank[7][0:T, D:2 * D]),
                                        per_head(mix[0:T, 0]), ALU.mult)
                if t >= 2:
                    dve.wait_ge(attn_turned, t - 1)
                link(nc.vector.tensor_tensor(heads(attn[0:T, t % 2]), heads(bank[7][0:T, 0:D]),
                                             per_head(mix[0:T, 1]), ALU.mult))
                nc.vector.tensor_tensor(attn[0:T, t % 2], attn[0:T, t % 2], read[0:T],
                                        ALU.add).then_inc(attn_ready, 1)

            def residual(t):
                dve.wait_ge(wo_ready, t + 1)
                dve.wait_ge(h_bo_ready, t + 1)
                nc.vector.tensor_tensor(h2[0:T, t], bank[4][0:T, D:2 * D], h_bo[0:T, t % RING],
                                        ALU.add).then_inc(h2_ready, 1)
                dve.wait_ge(h2_ready, t + 1)
                layer_stats(h2[0:T, t], 2 + t % 2, stats2)

            def norm2(t):
                dve.wait_ge(rstd2, t + 1)
                nc.vector.tensor_scalar(xln2[0:T, t % 2], h2[0:T, t], mv[0:T, 2 + t % 2, 0:1],
                                        rstd[0:T, 2 + t % 2:3 + t % 2], ALU.subtract,
                                        ALU.mult).then_inc(xln2_ready, 1)

            def row_lo(t):
                dve.wait_ge(row_hi_ready, t + 1)
                nc.vector.scalar_tensor_tensor(out=rows[0:T, t, D:2 * D], in0=xln2[0:T, t % 2],
                                               scalar=X_SCALE, in1=rows[0:T, t, 0:D], op0=ALU.mult,
                                               op1=ALU.subtract).then_inc(row_lo_ready, 1)

            logit = sb("logit", [P, 8])

            def top2(t):
                dve.wait_ge(logits_ready, t + 1)
                link(nc.vector.tensor_scalar(logit[0:T], bank[7][0:T, 0:EXPERTS],
                                             1.0 / (X_SCALE * W_SCALE), None, ALU.mult))
                link(nc.vector.max(top[0:T, t], logit[0:T]))
                nc.vector.max_index(top_at[0:T, t], top[0:T, t], logit[0:T]).then_inc(top_done, 1)
                nc.vector.tensor_tensor(gate_gap[0:T, 0, t:t + 1], top[0:T, t, 1:2], top[0:T, t, 0:1],
                                        ALU.subtract).then_inc(gap_ready, 1)

            dve.wait_ge(consts_in, 13 * 16)
            dve.wait_ge(beta_exp, 1)
            link(nc.vector.tensor_scalar(keep[0:T, 0], keep[0:T, 1], 1.0, None, ALU.add))
            link(nc.vector.reciprocal(keep[0:T, 0], keep[0:T, 0]))
            nc.vector.tensor_scalar(keep[0:T, 1], keep[0:T, 0], -1.0, 1.0, ALU.mult, ALU.add)
            dve.wait_ge(gate_hi, 1)
            nc.vector.scalar_tensor_tensor(out=gate_pair[:, :, 1], in0=s_wg, scalar=W_SCALE,
                                           in1=gate_pair[:, :, 0], op0=ALU.mult,
                                           op1=ALU.subtract).then_inc(gate_pair_ready, 1)
            for s in range(STEPS):
                if s < NT:
                    embed_h(s)
                if 0 <= s - 2 < NT:
                    mask_and_max(s - 2)
                if 0 <= s - 1 < NT:
                    min_q(s - 1)
                if s < NT:
                    norm1(s)
                if 0 <= s - 3 < NT:
                    combine(s - 3)
                if 0 <= s - 4 < NT:
                    residual(s - 4)
                if 0 <= s - 1 < NT:
                    finish_sq(s - 1)
                if 0 <= s - 5 < NT:
                    top2(s - 5)
                if 0 <= s - 4 < NT:
                    norm2(s - 4)
                    row_lo(s - 4)

            def over(ap, *dims):
                return ap.broadcast_to([T, *dims])

            dve.wait_ge(route_in, 7 * 16)
            dve.wait_ge(top_done, NT)
            link(nc.vector.tensor_copy(top_f[0:T].rearrange("p k t -> p t k"), top_at[0:T, :, 0:2]))
            for k in range(2):
                link(nc.vector.tensor_tensor(
                    pick[0:T, k], over(s_iota[0:T].rearrange("p (a b) -> p a b", a=1), NT, 8),
                    over(top_f[0:T, k].rearrange("p (a b) -> p a b", b=1), NT, 8), ALU.is_equal))
            link(nc.vector.tensor_tensor(prod[0:T, 0], pick[0:T, 0], pick[0:T, 1], ALU.add))
            link(nc.vector.memset(member[0:T, NT:NT + 1], 0.0))
            nc.vector.tensor_tensor(member[0:T, 0:NT], prod[0:T, 0], s_valid[0:T],
                                    ALU.mult).then_inc(members_ready, 1)
            dve.wait_ge(gap_exp, NT)
            link(nc.vector.tensor_scalar(gates[0:T, 1], gate_gap[0:T, 1], 1.0, None, ALU.add))
            link(nc.vector.reciprocal(gates[0:T, 0], gates[0:T, 1]))
            nc.vector.tensor_tensor(gates[0:T, 1], gates[0:T, 0], gate_gap[0:T, 1], ALU.mult)
            id_col = rows[0:T, :, ID_AT:ID_AT + 2].bitcast(U32)
            gate_col = rows[0:T, :, GATE_AT:GATE_AT + 2].bitcast(F32)
            nc.vector.tensor_copy(id_col, s_tid[0:T].rearrange("p (a b) -> p a b", b=1))
            link(nc.vector.tensor_copy(gate_col, gates[0:T, 0].rearrange("p (a b) -> p a b", b=1)))

            dve.wait_ge(ranks_ready, 1)
            link(nc.vector.tensor_copy(rank[0:T], bank[7][0:T, 0:(NT + 1) * 8].rearrange(
                "p (a b) -> p a b", b=8)))
            link(nc.vector.tensor_tensor(
                tiles_cmp[0:T], over(rank[0:T, NT].rearrange("p (a b) -> p a b", b=1), 8, 10),
                over(s_steps[0:T, 0:10].rearrange("p (a b) -> p a b", a=1), 8, 10), ALU.is_gt))
            link(nc.vector.tensor_reduce(tiles_of[0:T, 0], tiles_cmp[0:T], AX_X, ALU.add))
            link(nc.vector.tensor_tensor(
                tri[0:T], over(tiles_of[0:T, 0].rearrange("p (a b) -> p a b", a=1), 8, 8),
                s_lower[0:T], ALU.mult))
            link(nc.vector.tensor_reduce(tiles_of[0:T, 1], tri[0:T], AX_X, ALU.add))
            link(nc.vector.tensor_tensor(tiles_of[0:T, 2], tiles_of[0:T, 1], tiles_of[0:T, 0], ALU.add))
            link(nc.vector.tensor_scalar(tiles_of[0:T, 1], tiles_of[0:T, 1], float(P), None, ALU.mult))
            link(nc.vector.tensor_tensor(
                rank[0:T, 0:NT], rank[0:T, 0:NT],
                over(tiles_of[0:T, 1].rearrange("p (a b) -> p a b", a=1), NT, 8), ALU.add))
            for k in range(2):
                link(nc.vector.tensor_tensor(prod[0:T, k], rank[0:T, 0:NT], pick[0:T, k], ALU.mult))
            for k in range(2):
                link(nc.vector.tensor_reduce(slot_f[0:T, k], prod[0:T, k], AX_X, ALU.add))
            nc.vector.tensor_copy(slot_of[0:T], slot_f[0:T]).then_inc(slots_known, 1)
            link(nc.vector.tensor_tensor(
                end_cmp[0:T], over(tiles_of[0:T, 2].rearrange("p (a b) -> p a b", a=1), SLOT_TILES, 8),
                over(s_steps[0:T, 10:].rearrange("p (a b) -> p a b", b=1), SLOT_TILES, 8), ALU.is_le))
            link(nc.vector.tensor_reduce(exp_f[0:T, 0], end_cmp[0:T], AX_X, ALU.add))
            link(nc.vector.tensor_scalar(exp_f[0:T, 1], exp_f[0:T, 0], EXPERTS - 1.0, 1.0, ALU.min, ALU.add))
            nc.vector.tensor_scalar(expert_of[0:T], exp_f[0:T, 1], float(EW), None,
                                    ALU.mult).then_inc(experts_known, 1)

            def split_hidden(n, b, m, first=False):
                for half_ in range(2):
                    dve.wait_ge(hid_acted, 2 * n + half_ + 1)
                    if not first and half_ == 0:
                        dve.wait_ge(y_ready, n - 1)
                    src = act_out[:, half_].rearrange("p (a b) -> p a b", b=P)[:, :, 0:m]

                    def four(ap):
                        return ap[:, b, half_ * 512:half_ * 512 + 512].rearrange(
                            "p (a b) -> p a b", b=P)[:, :, 0:m]

                    nc.vector.tensor_scalar(four(hid_hi), src, H_SCALE, None, ALU.mult).then_inc(hi_ready, 1)
                    dve.wait_ge(hi_ready, 2 * n + half_ + 1)
                    nc.vector.scalar_tensor_tensor(out=four(hid_lo), in0=src, scalar=H_SCALE,
                                                   in1=four(hid_hi), op0=ALU.mult,
                                                   op1=ALU.subtract).then_inc(lo_ready, 1)

            def split_lo(c, at):
                dve.wait_ge(w_hi, c + 1)
                nc.vector.scalar_tensor_tensor(out=lo_of(c), in0=stage[:, at % STAGES], scalar=W_SCALE,
                                               in1=hi_of(c), op0=ALU.mult,
                                               op1=ALU.subtract).then_inc(w_lo_late, 1)

            def shared_y(t, b):
                dve.wait_ge(y_ready, t + 1)
                if t >= 3:
                    dve.wait_ge(shared_out[t % 3], 16 * (t // 3))
                nc.vector.scalar_tensor_tensor(out=y[0:T, t % 3], in0=bank[5 + b][0:T, 0:D],
                                               scalar=1.0 / (H_SCALE * W_SCALE), in1=h2[0:T, t],
                                               op0=ALU.mult, op1=ALU.add).then_inc(y_scaled, 1)

            split_hidden(0, 0, T, first=True)
            for t in range(1, NT):
                split_hidden(t, t % 2, T, first=(t == 1))
                if 2 <= t < NT - 1:
                    per = LOOP_CHUNKS // (NT - 3)
                    for c in range(FRONT_CHUNKS + per * (t - 2), FRONT_CHUNKS + per * (t - 1)):
                        split_lo(c, c)
                shared_y(t - 1, (t - 1) % 2)
                if t == 3:
                    dve.wait_ge(scattered[0], 16 * NT)
                    nc.vector.tensor_copy(gate_col, gates[0:T, 1].rearrange(
                        "p (a b) -> p a b", b=1)).then_inc(second_gates, 1)

            def slot_y(n, b, r):
                dve.wait_ge(y_ready, n + 1)
                nc.vector.tensor_scalar(y[:, b], bank[5 + b][:, 0:D],
                                        slot_rows[:, r, GATE_AT:GATE_AT + 2].bitcast(F32),
                                        1.0 / (H_SCALE * W_SCALE), ALU.mult,
                                        ALU.mult).then_inc(y_scaled, 1)

            split_hidden(NT, NT % 2, P)
            shared_y(NT - 1, (NT - 1) % 2)
            for q in range(3):
                dve.wait_ge(shared_out[q], 16 * len(range(q, NT, 3)))
            split_hidden(NT + 1, (NT + 1) % 2, P)
            slot_y(NT, NT % 2, 0)
            split_hidden(NT + 2, NT % 2, P)
            slot_y(NT + 1, (NT + 1) % 2, 1)

            def slot_step(j, r):
                split_hidden(NT + j, (NT + r) % 2, P)
                dve.wait_ge(added, 16 * (j - 2))
                slot_y(NT + j - 1, (NT + r + 1) % 2, (r + 3) % 4)

            SLOT_LOOP = (SLOT_TILES - 3) // 4
            with dve.Fori(0, SLOT_LOOP) as i:
                for r in range(3, 7):
                    slot_step(4 * i + r, r % 4)
            for j in range(4 * SLOT_LOOP + 3, SLOT_TILES):
                slot_step(j, j % 4)
            dve.wait_ge(added, 16 * (SLOT_TILES - 2))
            slot_y(NT + SLOT_TILES - 1, (NT + SLOT_TILES - 1) % 2, (SLOT_TILES - 1) % 4)


def kernel(x, cls_tok, L0_tok_W, L0_tok_b, L0_attn_Wq, L0_attn_Wk, L0_attn_Wv, L0_attn_Wo, L0_attn_bo,
           L0_attn_betas, L0_attn_mem, L0_attn_z, L0_ffn_shared_w1, L0_ffn_shared_w2,
           L0_ffn_experts_w1, L0_ffn_experts_w2, L0_ffn_gate_w):
    import numpy as np
    import concourse.bacc as bacc
    from concourse.bass_utils import run_bass_kernel_spmd

    f32 = np.float32

    def fold(w):
        k, n = w.shape
        return w.reshape(k // P, P, n).transpose(1, 0, 2).reshape(P, -1)

    px = np.asarray(x).reshape(IMAGES, 3, 6, 16, 6, 16).transpose(0, 2, 4, 1, 3, 5).reshape(IMAGES, 36, PATCH)
    padded = np.zeros((NT * PER_TILE, SEQ, PATCH), f32)
    padded[:IMAGES, 1:] = px
    patches = padded.reshape(NT, T, PC, P).transpose(0, 3, 2, 1).reshape(NT, P, PC * T)

    eb = np.concatenate([np.asarray(cls_tok).reshape(1, D), np.broadcast_to(L0_tok_b, (SEQ - 1, D))])
    embed_bias = np.concatenate([eb] * PER_TILE)
    wq, wk = np.asarray(L0_attn_Wq).T, np.asarray(L0_attn_Wk).T
    w_qk = np.concatenate([wq, wk], axis=1)
    mem = np.zeros((P, KC, P), f32)
    z = np.zeros((P, KC, 2), f32)
    for hd in range(HEADS):
        at = slice(HD * (hd % 2), HD * (hd % 2) + HD)
        mem[at, hd // 2, at] = L0_attn_mem[hd]
        z[at, hd // 2, hd % 2] = np.asarray(L0_attn_z)[hd, :, 0]
    w1 = np.concatenate([np.asarray(L0_ffn_shared_w1)[None], np.asarray(L0_ffn_experts_w1)])
    w2 = np.concatenate([np.asarray(L0_ffn_shared_w2)[None], np.asarray(L0_ffn_experts_w2)])
    n = EXPERTS + 1
    w1 = w1.transpose(0, 2, 1).reshape(n, KC, P, HIDDEN).transpose(0, 2, 1, 3).reshape(n, P, KC * HIDDEN)
    w2 = w2.transpose(0, 2, 1).reshape(n, HC, P, D).transpose(0, 2, 1, 3).reshape(n, P, HC * D)

    tok = np.arange(T)
    same = tok[:, None] // SEQ == tok[None, :] // SEQ
    causal = np.where(same & (tok[None, :] <= tok[:, None]), 0.0, -1e30).astype(f32)
    pad_rows = np.zeros((P, ROW // 2), np.uint32)
    pad_rows[:, ID_AT // 2] = TOKENS + np.arange(P)
    token_id = (np.arange(NT)[None, :] * T + tok[:, None]).astype(np.uint32)
    valid = np.broadcast_to((token_id < TOKENS)[:, :, None], (T, NT, 8)).astype(f32)
    steps = np.concatenate([P * np.arange(10), np.arange(SLOT_TILES)]).astype(f32)

    ins = dict(
        patches=patches, w_embed=fold(np.asarray(L0_tok_W).T), embed_bias=embed_bias, w_qk=fold(w_qk),
        w_v=fold(np.asarray(L0_attn_Wv).T), w_o=fold(np.asarray(L0_attn_Wo).T),
        out_bias=np.broadcast_to(L0_attn_bo, (T, D)),
        betas=np.broadcast_to(np.asarray(L0_attn_betas).reshape(1, HEADS), (T, HEADS)),
        mem=mem.reshape(P, -1), z=z.reshape(P, -1), w_ffn=np.concatenate([w1, w2], axis=2),
        w_gate=fold(np.asarray(L0_ffn_gate_w).T),
        ident=np.eye(P, dtype=f32), ident16=np.eye(P, dtype=np.float16), causal=causal,
        before=(tok[:, None] < tok[None, :]).astype(np.float16), valid=valid, token_id=token_id,
        pad_rows=pad_rows,
        lower=np.broadcast_to((np.arange(8)[None, :] < np.arange(8)[:, None]).astype(f32), (T, 8, 8)),
        iota=np.broadcast_to(np.arange(8, dtype=f32), (T, 8)), steps=np.broadcast_to(steps, (T, len(steps))))

    nc = bacc.Bacc("TRN2", target_bir_lowering=False, num_devices=1)
    arrays, args = {}, {}
    for name, a in ins.items():
        a = np.ascontiguousarray(a)
        arrays[f"in_{name}"] = a
        args[name] = nc.dram_tensor(f"in_{name}", a.shape, mybir.dt.from_np(a.dtype), kind="ExternalInput").ap()
    out = nc.dram_tensor("out_rows", (TOKENS + P, D), F32, kind="ExternalOutput").ap()
    build(nc, **args, out=out)
    r = run_bass_kernel_spmd(nc, [arrays], core_ids=[0])
    return r.results[0]["out_rows"][:TOKENS].reshape(IMAGES, SEQ, D)
```

```python
from contextlib import ExitStack

import concourse.bass as bass
from concourse import mybir

ALU = mybir.AluOpType
ACT = mybir.ActivationFunctionType
F32 = mybir.dt.float32
F16 = mybir.dt.float16
U32 = mybir.dt.uint32
I32 = mybir.dt.int32
AX_X = mybir.AxisListType.X

P = 128
IMAGES, SEQ, D = 32, 37, 256
PER_TILE = 3
T = PER_TILE * SEQ
NT = -(-IMAGES // PER_TILE)
TOKENS = IMAGES * SEQ
LAST = TOKENS - (NT - 1) * T
HEADS, HD = 4, 64
KC = D // P
PATCH = 768
PC = PATCH // P
EXPERTS, HIDDEN = 8, 1024
HC = HIDDEN // P
SLOT_TILES = (2 * TOKENS + EXPERTS * (P - 1)) // P
EPS = 1e-5
ROUND = 1.5 * 2.0 ** 23
X_SCALE, W_SCALE, H_SCALE, G_SCALE = 64.0, 64.0, 16.0, 2.0 ** 14
CHUNK = 1024
CHUNKS = 4
EW = CHUNKS * 2 * CHUNK
STAGES = 6
EARLY = 4
RING = 5


def build(nc, patches, w_embed, embed_bias, w_qk, w_v, w_o, out_bias, betas, mem, z, w_ffn, w_gate,
          ident, ident16, causal, before, valid, token_id, dummy_id, lower, iota, steps, out):
    x_rows = nc.dram_tensor("x_rows", [NT * T, 2 * D], F16, kind="Internal").ap()

    with ExitStack() as ctx:
        def sb(name, shape, dt=F32):
            return ctx.enter_context(nc.sbuf_tensor(name, shape, dt))

        def sem(name):
            return ctx.enter_context(nc.semaphore(name))

        bank = [ctx.enter_context(nc.psum_tensor(f"bank{i}", [P, 512], F32)) for i in range(8)]

        weights = sb("weights", [P, (EXPERTS + 1) * EW], F16)
        stage = sb("stage", [P, STAGES, CHUNK])
        rows = sb("rows", [P, NT, 2 * D], F16)
        id16 = sb("id16", [P, P], F16)
        gate_pair = sb("gate_pair", [P, KC, 2, EXPERTS], F16)
        top = sb("top", [P, NT, 8])
        top_at = sb("top_at", [P, NT, 8], U32)
        gates = sb("gates", [P, 2, NT])
        gate_gap = sb("gate_gap", [P, 2, NT])
        slot_gate = sb("slot_gate", [P, SLOT_TILES])
        gather_id = sb("gather_id", [P, SLOT_TILES], U32)
        add_id = sb("add_id", [P, SLOT_TILES], U32)
        expert_of = sb("expert_of", [P, SLOT_TILES], I32)

        slot_rows = sb("slot_rows", [P, 4, 2 * D], F16)
        x_t = sb("x_t", [P, 2, 4 * P], F16)
        act_out = sb("act_out", [P, 2, 512])
        hid_hi = sb("hid_hi", [P, 2, HIDDEN], F16)
        hid_lo = sb("hid_lo", [P, 2, HIDDEN], F16)
        y = sb("y", [P, 3, D])

        space = weights[:, EARLY * EW:].bitcast(F32)
        used = [0]

        def part(*dims):
            n = 1
            for d in dims:
                n *= d
            ap = space[:, used[0]:used[0] + n]
            used[0] += n
            assert used[0] <= (EXPERTS + 1 - EARLY) * EW // 2
            if len(dims) == 2:
                return ap.rearrange("p (a b) -> p a b", b=dims[1])
            if len(dims) == 3:
                return ap.rearrange("p (a b c) -> p a b c", b=dims[1], c=dims[2])
            return ap

        s_we = part(PC, D)
        s_wqk = part(KC, 4, P)
        s_wv = part(KC, D)
        s_wo = part(KC, D)
        s_eb = part(D)
        s_ob = part(D)
        s_id = part(P)
        s_causal = part(T).bitcast(mybir.dt.bfloat16)
        s_beta = part(HEADS)
        s_mem = part(KC, P)
        s_z = part(KC, 2)
        s_wg = part(KC, EXPERTS)
        keep = part(2 * HEADS)
        s_patch = part(2, PC, T)
        h = part(RING, D)
        h_bo = part(RING, D)
        xln = part(2, D)
        xln_t = part(2, KC, T)
        qk_t = part(2, 4, T)
        v = part(3, D)
        q_min = part(2, 2, T)
        sq = part(3, 2, T)
        prob = part(2, HEADS * T)
        prob_t = part(2, HEADS * T)
        neg_max = part(2, HEADS)
        mix = part(4, 2 * HEADS)
        share = part(2 * HEADS)
        read = sb("read", [P, D])[:]
        attn = part(2, D)
        attn_t = part(2, KC, T)
        xln2 = part(2, D)
        h2 = part(4, D)
        x2_t = part(2, 4 * T // 2)
        stats = part(2, 6)
        mv = part(4, 2)
        rstd = part(4)
        newton = part(4)
        shift = part(4)
        q_num = part(2, T)
        q_den = part(2, T)
        var_eps = part(4)
        half = part(1)

        table_words = 2 * NT * (P + 5 * SLOT_TILES) // 2
        tables = space[:, (EXPERTS + 1 - EARLY) * EW // 2 - table_words:].bitcast(F16)
        assert used[0] <= (EXPERTS + 1 - EARLY) * EW // 2 - table_words
        in_row = tables[:, 0:2 * NT * P].rearrange("p (a b) -> p a b", b=P)
        in_tile = tables[:, 2 * NT * P:].rearrange("p (a c b) -> p a c b", c=5, b=SLOT_TILES)
        gate_rest = sb("gate_rest", [P, 2, NT])
        gate_parts = sb("gate_parts", [P, 3, 2, NT], F16)
        gate_sum = sb("gate_sum", [P, SLOT_TILES])
        s_before = sb("s_before", [P, T], F16)
        ones = sb("ones", [P, T], F16)
        s_valid = sb("s_valid", [P, NT])
        s_tid = sb("s_tid", [P, NT])
        s_dummy = sb("s_dummy", [P, 1])
        s_lower = sb("s_lower", [P, 8, 8])
        s_iota = sb("s_iota", [P, P])
        s_steps = sb("s_steps", [P, 10])
        top_f = sb("top_f", [P, 2, NT])
        temp = y[:].rearrange("p a b -> p (a b)")
        rank = temp[:, 0:96].rearrange("p (a b) -> p a b", b=8)
        pick = temp[:, 96:272].rearrange("p (k a b) -> p k a b", k=2, b=8)
        prod = temp[:, 272:448].rearrange("p (k a b) -> p k a b", k=2, b=8)
        tiles_cmp = temp[:, 448:528].rearrange("p (a b) -> p a b", b=10)
        tri = temp[:, 528:592].rearrange("p (a b) -> p a b", b=8)
        end_cmp = temp[:, 272:272 + 8 * SLOT_TILES].rearrange("p (a b) -> p a b", b=8)
        member = sb("member", [P, NT + 1, 8], F16)
        tiles_of = sb("tiles_of", [P, 3, 8])
        slot_f = sb("slot_f", [P, 3, 2 * NT])
        vacant = sb("vacant", [P, SLOT_TILES])
        exp_f = sb("exp_f", [P, 2, SLOT_TILES])

        embed_in = sem("embed_in")
        consts_in = sem("consts_in")
        attn_in = sem("attn_in")
        route_in = sem("route_in")
        patches_in = [sem(f"patches_in{i}") for i in range(2)]
        stage_in = [sem(f"stage_in{i}") for i in range(STAGES)]
        rows_out = sem("rows_out")
        h2_stored = [sem(f"h2_stored{i}") for i in range(4)]
        dummy_zero = sem("dummy_zero")
        dummy_out = sem("dummy_out")

        embed_ready = sem("embed_ready")
        h_ready = sem("h_ready")
        h_bo_ready = sem("h_bo_ready")
        stats1 = sem("stats1")
        rstd1 = sem("rstd1")
        stats2 = sem("stats2")
        rstd2 = sem("rstd2")
        pool_step = sem("pool_step")
        xln_ready = sem("xln_ready")
        xln_turned = sem("xln_turned")
        xln_t_ready = sem("xln_t_ready")
        qk_ready = sem("qk_ready")
        v_ready = sem("v_ready")
        qk_copied = sem("qk_copied")
        v_copied = sem("v_copied")
        q_min_ready = sem("q_min_ready")
        q_tanh_ready = sem("q_tanh_ready")
        q_terms_ready = sem("q_terms_ready")
        sq_ready = sem("sq_ready")
        scores_ready = sem("scores_ready")
        max_ready = sem("max_ready")
        prob_ready = sem("prob_ready")
        prob_turned = sem("prob_turned")
        prob_t_ready = sem("prob_t_ready")
        mixed_ready = sem("mixed_ready")
        dens_ready = sem("dens_ready")
        attn_ready = sem("attn_ready")
        attn_turned = sem("attn_turned")
        attn_t_ready = sem("attn_t_ready")
        wo_ready = sem("wo_ready")
        h2_ready = sem("h2_ready")
        row_hi_ready = sem("row_hi_ready")
        row_lo_ready = sem("row_lo_ready")
        x2_turned = sem("x2_turned")
        x2_t_ready = sem("x2_t_ready")
        logits_ready = sem("logits_ready")
        gap_ready = sem("gap_ready")
        gap_exp = sem("gap_exp")
        top_done = sem("top_done")
        beta_exp = sem("beta_exp")
        gate_hi = sem("gate_hi")
        gate_pair_ready = sem("gate_pair_ready")
        ones_ready = sem("ones_ready")
        dve_step = sem("dve_step")
        members_ready = sem("members_ready")
        ranks_ready = sem("ranks_ready")
        tile_hots_ready = sem("tile_hots_ready")
        tile_values_ready = sem("tile_values_ready")
        tables_ready = sem("tables_ready")
        inverse_ready = sem("inverse_ready")
        slots_known = sem("slots_known")
        experts_known = sem("experts_known")
        w_scaled = sem("w_scaled")
        w_hi = sem("w_hi")
        w_lo_pool = sem("w_lo_pool")
        w_lo_dve = sem("w_lo_dve")

        slot_rows_in = [sem(f"slot_rows_in{i}") for i in range(4)]
        x_turned = sem("x_turned")
        x_t_ready = sem("x_t_ready")
        hid_ready = sem("hid_ready")
        hid_acted = sem("hid_acted")
        hi_ready = sem("hi_ready")
        lo_ready = sem("lo_ready")
        y_ready = sem("y_ready")
        y_half = sem("y_half")
        y_scaled = sem("y_scaled")
        shared_out = [sem(f"shared_out{i}") for i in range(3)]
        added = sem("added")

        def staged(eng, c):
            eng.wait_ge(stage_in[c % STAGES], 16 * (c // STAGES + 1))

        NCHUNK = (EXPERTS + 1) * CHUNKS
        FRONT_CHUNKS = EARLY * CHUNKS
        STEPS = NT + 5
        LOOP_CHUNKS = NCHUNK - FRONT_CHUNKS

        def chunks_at(step):
            first, last = 1, STEPS - 1
            if not first <= step < last:
                return range(0)
            return range(FRONT_CHUNKS * (step - first) // (last - first),
                         FRONT_CHUNKS * (step + 1 - first) // (last - first))

        def late_at(t):
            if not 1 <= t < NT - 1:
                return range(0)
            return range(NCHUNK - LOOP_CHUNKS * (NT - 1 - t) // (NT - 2),
                         NCHUNK - LOOP_CHUNKS * (NT - 2 - t) // (NT - 2))

        def by_pool(c):
            return c % 2 == 0 if c < FRONT_CHUNKS else c % 5 in (1, 3)

        def taken(chunks, pool_side):
            return sum(by_pool(c) == pool_side for c in range(chunks))

        def wait_split(eng, chunks):
            for done, pool_side in ((w_lo_pool, True), (w_lo_dve, False)):
                if taken(chunks, pool_side):
                    eng.wait_ge(done, taken(chunks, pool_side))

        def pair_of(c, w):
            both = weights[:, bass.ds(2 * CHUNK * c, 2 * CHUNK)]
            return both.rearrange("p (g w d) -> p g w d", w=2, d=D)[:, :, w]

        def hi_of(c):
            return pair_of(c, 0)

        def lo_of(c):
            return pair_of(c, 1)

        def staged_of(c):
            return stage[:, c % STAGES].rearrange("p (g d) -> p g d", d=D)

        def w_rows(c):
            return w_ffn[c // CHUNKS, :, CHUNK * (c % CHUNKS):CHUNK * (c % CHUNKS + 1)]

        block = ctx.enter_context(nc.Block())

        S0 = NT

        @block.sync
        def _(sp):
            def load_chunk(c):
                last = c - STAGES
                if last >= 0:
                    sp.wait_ge(w_lo_pool if by_pool(last) else w_lo_dve,
                               taken(last + 1, by_pool(last)))
                sp.dma_start(stage[:, c % STAGES], w_rows(c)).then_inc(stage_in[c % STAGES], 16)

            def load_patches(t):
                if t >= 2:
                    sp.wait_ge(embed_ready, t - 1)
                sp.dma_start(s_patch[:, t % 2].rearrange("p a b -> p (a b)"),
                             patches[t]).then_inc(patches_in[t % 2], 16)

            load_patches(0)
            sp.dma_start(s_we.rearrange("p a b -> p (a b)"), w_embed).then_inc(embed_in, 16)
            for dst, src in ((s_eb[0:T], embed_bias), (s_id, ident),
                             (s_wqk.rearrange("p a b c -> p (a b c)"), w_qk),
                             (s_wv.rearrange("p a b -> p (a b)"), w_v), (s_ob[0:T], out_bias)):
                sp.dma_start(dst, src).then_inc(consts_in, 16)
            load_patches(1)
            for dst, src in ((s_causal[0:T], causal), (id16[:], ident16), (s_beta[0:T], betas),
                             (s_mem.rearrange("p a b -> p (a b)"), mem),
                             (s_z.rearrange("p a b -> p (a b)"), z),
                             (s_wo.rearrange("p a b -> p (a b)"), w_o),
                             (s_wg.rearrange("p a b -> p (a b)"), w_gate)):
                sp.dma_start(dst, src).then_inc(attn_in, 16)
            for dst, src in ((s_before[0:T], before), (s_valid[0:T], valid), (s_tid[0:T], token_id),
                             (s_dummy[:], dummy_id), (s_lower[0:T], lower), (s_iota[:], iota),
                             (s_steps[0:T], steps)):
                sp.dma_start(dst, src).then_inc(route_in, 16)
            sp.wait_ge(dummy_zero, 1)
            sp.dma_start(out[TOKENS:TOKENS + P], y[:, 2]).then_inc(dummy_out, 16)
            loaded = 0
            for step in range(STEPS + 1):
                if step + 2 < NT:
                    load_patches(step + 2)
                while loaded < min(chunks_at(step).stop + 2, FRONT_CHUNKS):
                    load_chunk(loaded)
                    loaded += 1
                t = step - 5
                if 0 <= t < NT:
                    m = T if t < NT - 1 else LAST
                    sp.wait_ge(h2_ready, t + 1)
                    sp.dma_start(out[t * T:t * T + m], h2[0:m, t % 4]).then_inc(h2_stored[t % 4], 16)
                    sp.wait_ge(row_lo_ready, t + 1)
                    sp.dma_start(x_rows[t * T:(t + 1) * T], rows[0:T, t]).then_inc(rows_out, 16)
            for c in range(FRONT_CHUNKS, NCHUNK):
                load_chunk(c)

        @block.tensor
        def _(pe):
            def scores(t):
                pe.wait_ge(qk_copied, t + 1)
                if t == 0:
                    pe.wait_ge(attn_in, 7 * 16)
                if t >= 1:
                    pe.wait_ge(prob_ready, t)
                if t >= 2:
                    pe.wait_ge(attn_ready, t - 1)
                for odd in range(2):
                    nc.tensor.matmul(bank[7 * odd][0:T, 0:2 * T], id16[0:T, 0:T], s_causal[0:T],
                                     start=True, stop=False)
                for hd in range(HEADS):
                    at = slice(HD * (hd % 2), HD * (hd % 2) + HD)
                    to = bank[7 * (hd % 2)][0:T, (hd // 2) * T:(hd // 2 + 1) * T]
                    mm = nc.tensor.matmul(to, qk_t[at, t % 2, hd // 2],
                                          qk_t[at, t % 2, 2 + hd // 2], start=False, stop=(hd >= 2))
                mm.then_inc(scores_ready, 1)

            def turn_prob(t):
                pe.wait_ge(prob_ready, t + 1)
                if t >= 1:
                    pe.wait_ge(prob_t_ready, t)
                for hd in range(HEADS):
                    mm = nc.tensor.transpose(bank[2][0:T, hd * T:(hd + 1) * T],
                                             prob[0:T, t % 2, hd * T:(hd + 1) * T], s_id[0:T, 0:T])
                mm.then_inc(prob_turned, 1)

            def turn_attn(t):
                pe.wait_ge(attn_ready, t + 1)
                if t >= 1:
                    pe.wait_ge(attn_t_ready, t)
                if t >= 2:
                    pe.wait_ge(x2_t_ready, t - 1)
                for k in range(KC):
                    mm = nc.tensor.transpose(bank[3][:, k * T:(k + 1) * T],
                                             attn[0:T, t % 2, k * P:(k + 1) * P], s_id[0:T, 0:T])
                mm.then_inc(attn_turned, 1)

            def turn_xln(t):
                pe.wait_ge(xln_ready, t + 1)
                if t == 0:
                    pe.wait_ge(consts_in, 5 * 16)
                if t >= 1:
                    pe.wait_ge(xln_t_ready, t)
                if t >= 3:
                    pe.wait_ge(dens_ready, t - 2)
                for k in range(KC):
                    mm = nc.tensor.transpose(bank[1][:, k * T:(k + 1) * T],
                                             xln[0:T, t % 2, k * P:(k + 1) * P], s_id[0:T, 0:T])
                mm.then_inc(xln_turned, 1)

            def embed(t):
                if t == 0:
                    pe.wait_ge(embed_in, 16)
                pe.wait_ge(patches_in[t % 2], 16 * (t // 2 + 1))
                if t >= 5:
                    pe.wait_ge(h2_ready, t - 4)
                if t >= 1:
                    pe.wait_ge(h_ready, t)
                for k in range(PC):
                    mm = nc.tensor.matmul(bank[4][0:T, 0:D], s_patch[:, t % 2, k], s_we[:, k],
                                          start=(k == 0), stop=(k == PC - 1))
                mm.then_inc(embed_ready, 1)

            def turn_rows(t):
                pe.wait_ge(row_lo_ready, t + 1)
                pe.wait_ge(attn_t_ready, min(t + 2, NT))
                if t >= 1:
                    pe.wait_ge(x2_t_ready, t)
                for q in range(4):
                    mm = nc.tensor.transpose(bank[3][:].bitcast(F16)[:, q * 128:q * 128 + T],
                                             rows[0:T, t, q * P:(q + 1) * P], id16[0:T, 0:T])
                mm.then_inc(x2_turned, 1)

            def project(t):
                pe.wait_ge(xln_t_ready, t + 1)
                if t >= 1:
                    pe.wait_ge(qk_copied, t)
                for o in range(4):
                    for k in range(KC):
                        mm = nc.tensor.matmul(bank[5][:, o * T:(o + 1) * T], s_wqk[:, k, o],
                                              xln_t[:, t % 2, k], start=(k == 0), stop=(k == KC - 1))
                mm.then_inc(qk_ready, 1)
                if t >= 1:
                    pe.wait_ge(v_copied, t)
                if t >= 5:
                    pe.wait_ge(top_done, t - 4)
                for k in range(KC):
                    mm = nc.tensor.matmul(bank[6][0:T, 0:D], xln_t[:, t % 2, k], s_wv[:, k],
                                          start=(k == 0), stop=(k == KC - 1))
                mm.then_inc(v_ready, 1)

            def mix_values(t):
                pe.wait_ge(prob_t_ready, t + 1)
                pe.wait_ge(v_copied, t + 1)
                pe.wait_ge(sq_ready, t + 1)
                pe.wait_ge(prob_ready, min(t + 2, NT))
                for hd in range(HEADS):
                    nc.tensor.matmul(bank[7][0:T, hd * HD:(hd + 1) * HD],
                                     prob_t[0:T, t % 2, hd * T:(hd + 1) * T],
                                     v[0:T, t % 3, hd * HD:(hd + 1) * HD], start=True, stop=True)
                for k in range(KC):
                    nc.tensor.matmul(bank[7][0:T, D + k * P:D + (k + 1) * P], sq[:, t % 3, k],
                                     s_mem[:, k], start=True, stop=True)
                pe.wait_ge(xln_t_ready, min(t + 3, NT))
                for k in range(KC):
                    mm = nc.tensor.matmul(bank[1][0:T, 2 * k:2 * k + 2], sq[:, t % 3, k],
                                          s_z[:, k], start=True, stop=True)
                mm.then_inc(mixed_ready, 1)

            def project_out(t):
                pe.wait_ge(attn_t_ready, t + 1)
                pe.wait_ge(h_ready, min(t + 5, NT))
                if t >= 1:
                    pe.wait_ge(h2_ready, t)
                for k in range(KC):
                    mm = nc.tensor.matmul(bank[4][0:T, D:2 * D], attn_t[:, t % 2, k], s_wo[:, k],
                                          start=(k == 0), stop=(k == KC - 1))
                mm.then_inc(wo_ready, 1)

            def logits(t):
                pe.wait_ge(x2_t_ready, t + 1)
                if t == 0:
                    pe.wait_ge(gate_pair_ready, 1)
                pe.wait_ge(v_copied, min(t + 5, NT))
                if t >= 1:
                    pe.wait_ge(top_done, t)
                turned = x2_t[:, t % 2].bitcast(F16)
                prods = [(0, 0), (0, 1), (1, 0)]
                for k in range(KC):
                    for n, (a, b) in enumerate(prods):
                        q = 2 * a + k
                        mm = nc.tensor.matmul(bank[6][0:T, D:D + EXPERTS], turned[:, q * T:(q + 1) * T],
                                              gate_pair[:, k, b], start=(k == 0 and n == 0),
                                              stop=(k == KC - 1 and n == 2))
                mm.then_inc(logits_ready, 1)

            for s in range(STEPS):
                if 0 <= s - 3 < NT:
                    turn_prob(s - 3)
                if 0 <= s - 1 < NT:
                    turn_xln(s - 1)
                if s < NT:
                    embed(s)
                if 0 <= s - 4 < NT:
                    turn_attn(s - 4)
                if 0 <= s - 2 < NT:
                    scores(s - 2)
                if 0 <= s - 1 < NT:
                    project(s - 1)
                if 0 <= s - 4 < NT:
                    project_out(s - 4)
                if 0 <= s - 5 < NT:
                    turn_rows(s - 5)
                if 0 <= s - 3 < NT:
                    mix_values(s - 3)
                if 0 <= s - 5 < NT:
                    logits(s - 5)

            def ranks():
                pe.wait_ge(members_ready, 1)
                pe.wait_ge(route_in, 7 * 16)
                pe.wait_ge(ones_ready, 1)
                flat = bank[7][0:T, 0:(NT + 1) * 8]
                nc.tensor.matmul(flat, s_before[0:T, :], member[0:T].rearrange("p a b -> p (a b)"),
                                 start=True, stop=False)
                for t in range(NT):
                    later = flat[:, (t + 1) * 8:].rearrange("p (a b) -> p a b", b=8)
                    src = member[0:T, t:t + 1, :].broadcast_to([T, NT - t, 8])
                    mm = nc.tensor.matmul(later, ones[0:T, :], src, start=False, stop=(t == NT - 1))
                mm.then_inc(ranks_ready, 1)

            def inverse():
                pe.wait_ge(tables_ready, 1)
                pe.wait_ge(tile_values_ready, 1)
                for a in range(2 * NT):
                    mm = nc.tensor.matmul(bank[7][:, 0:5 * SLOT_TILES], in_row[0:T, a],
                                          in_tile[0:T, a].rearrange("p c b -> p (c b)"),
                                          start=(a == 0), stop=(a == 2 * NT - 1))
                mm.then_inc(inverse_ready, 1)

            def turn(n, b, src, m):
                for q in range(4):
                    mm = nc.tensor.transpose(bank[4][:].bitcast(F16)[:, q * P:q * P + m],
                                             src[0:m, q * P:(q + 1) * P], id16[0:m, 0:m])
                mm.then_inc(x_turned, 1)

            def up(n, b, m, base):
                pe.wait_ge(x_t_ready, n + 1)
                for half_ in range(2):
                    for c in range(4):
                        o = bank[2 * b + half_][:, c * P:c * P + m]
                        col = (4 * half_ + c) * P
                        for k in range(KC):
                            for w, x in ((0, 0), (0, 1), (1, 0)):
                                mm = nc.tensor.matmul(
                                    o, weights[:, bass.ds(base + 2 * k * CHUNK + 2 * (col - col % D)
                                                          + w * D + col % D, P)],
                                    x_t[:, b, (2 * x + k) * P:(2 * x + k) * P + m],
                                    start=(k == 0 and w + x == 0), stop=(k == 1 and w == 1))
                    mm.then_inc(hid_ready, 1)

            def down(n, b, m, base):
                for c in range(HC):
                    if c % 4 == 0:
                        pe.wait_ge(lo_ready, 2 * n + c // 4 + 1)
                    at = base + 2 * KC * CHUNK + c * 2 * D
                    nc.tensor.matmul(bank[5 + b][0:m, :], hid_hi[:, b, c * P:c * P + m],
                                     weights[:, bass.ds(at, 2 * D)], start=(c == 0), stop=False)
                    mm = nc.tensor.matmul(bank[5 + b][0:m, 0:D], hid_lo[:, b, c * P:c * P + m],
                                          weights[:, bass.ds(at, D)], start=False, stop=(c == HC - 1))
                mm.then_inc(y_ready, 1)

            pe.wait_ge(h2_ready, NT)
            turn(0, 0, rows[:, 0], T)
            pe.wait_ge(attn_ready, NT)
            pe.wait_ge(x2_t_ready, NT)
            wait_split(pe, CHUNKS)
            up(0, 0, T, 0)
            ranks()
            turn(1, 1, rows[:, 1], T)
            up(1, 1, T, 0)
            turn(2, 0, rows[:, 2], T)
            down(0, 0, T, 0)

            def shared_pair(n):
                for b in range(2):
                    up(n + b, b, T, 0)
                    turn(n + b + 1, 1 - b, rows[:, bass.ds(n + b + 1, 1)].rearrange("p a b -> p (a b)"), T)
                    down(n + b - 1, 1 - b, T, 0)

            with pe.Fori(1, 3) as i:
                shared_pair(2 * i)
            inverse()
            with pe.Fori(3, (NT - 1) // 2) as i:
                shared_pair(2 * i)
            up(NT - 1, 0, T, 0)

            def expert(j):
                return pe.value_load(expert_of[0:1, bass.ds(j, 1)], min_val=EW, max_val=EXPERTS * EW)

            def rows_of(j, r, quad):
                pe.wait_ge(slot_rows_in[r], 16 * (quad + 1))
                turn(NT + j, (NT + r) % 2, slot_rows[:, r], P)

            rows_of(0, 0, 0)
            down(NT - 2, 1, T, 0)
            pe.wait_ge(experts_known, 1)
            wait_split(pe, NCHUNK)
            up(NT, NT % 2, P, expert(0))
            rows_of(1, 1, 0)
            down(NT - 1, 0, T, 0)

            def slot_step(j, r, quad_next, last_expert):
                this_expert = expert(j)
                up(NT + j, (NT + r) % 2, P, this_expert)
                if quad_next is not None:
                    rows_of(j + 1, (r + 1) % 4, quad_next)
                down(NT + j - 1, (NT + r + 1) % 2, P, last_expert)
                return this_expert

            last = expert(0)
            for j in range(1, SLOT_TILES):
                last = slot_step(j, j % 4, (j + 1) // 4 if j + 1 < SLOT_TILES else None, last)
            down(NT + SLOT_TILES - 1, (NT + SLOT_TILES - 1) % 2, P, last)

        @block.scalar
        def _(act):
            def exps(t):
                act.wait_ge(max_ready, t + 1)
                if t >= 2:
                    act.wait_ge(prob_turned, t - 1)
                for hd in range(HEADS):
                    src = bank[7 * (hd % 2)][0:T, (hd // 2) * T:(hd // 2 + 1) * T]
                    top_ = 2 * (hd % 2) + hd // 2
                    last = nc.scalar.activation(prob[0:T, t % 2, hd * T:(hd + 1) * T], src, ACT.Exp,
                                                bias=neg_max[0:T, t % 2, top_:top_ + 1],
                                                accum_out=mix[0:T, t % 4, HEADS + hd:HEADS + hd + 1])
                last.then_inc(prob_ready, 1)

            def copy_xln_t(t):
                act.wait_ge(xln_turned, t + 1)
                if t >= 2:
                    act.wait_ge(v_ready, t - 1)
                nc.scalar.copy(xln_t[:, t % 2].rearrange("p a b -> p (a b)"),
                               bank[1][:, 0:KC * T]).then_inc(xln_t_ready, 1)

            def copy_prob_t(t):
                act.wait_ge(prob_turned, t + 1)
                if t >= 2:
                    act.wait_ge(mixed_ready, t - 1)
                nc.scalar.copy(prob_t[0:T, t % 2], bank[2][0:T, 0:HEADS * T]).then_inc(prob_t_ready, 1)

            def copy_attn_t(t):
                act.wait_ge(attn_turned, t + 1)
                if t >= 2:
                    act.wait_ge(wo_ready, t - 1)
                nc.scalar.copy(attn_t[:, t % 2].rearrange("p a b -> p (a b)"),
                               bank[3][:, 0:KC * T]).then_inc(attn_t_ready, 1)

            def copy_x2_t(t):
                act.wait_ge(x2_turned, t + 1)
                if t >= 2:
                    act.wait_ge(logits_ready, t - 1)
                nc.scalar.copy(x2_t[:, t % 2].bitcast(F16).rearrange("p (a b) -> p a b", b=T),
                               bank[3][:].bitcast(F16)[:, 0:512].rearrange("p (a b) -> p a b", b=128)[:, :, 0:T]
                               ).then_inc(x2_t_ready, 1)

            def copy_qkv(t):
                act.wait_ge(qk_ready, t + 1)
                if t >= 2:
                    act.wait_ge(scores_ready, t - 1)
                nc.scalar.copy(qk_t[:, t % 2].rearrange("p a b -> p (a b)"),
                               bank[5][:, 0:4 * T]).then_inc(qk_copied, 1)
                act.wait_ge(v_ready, t + 1)
                if t >= 3:
                    act.wait_ge(mixed_ready, t - 2)
                nc.scalar.copy(v[0:T, t % 3], bank[6][0:T, 0:D]).then_inc(v_copied, 1)

            def tanh_q(t):
                act.wait_ge(q_min_ready, t + 1)
                nc.scalar.activation(q_min[:, t % 2].rearrange("p a b -> p (a b)"),
                                     q_min[:, t % 2].rearrange("p a b -> p (a b)"),
                                     ACT.Tanh, scale=0.5).then_inc(q_tanh_ready, 1)

            def split_hi(c):
                if by_pool(c):
                    act.wait_ge(w_scaled, taken(c + 1, True))
                    nc.scalar.copy(hi_of(c), staged_of(c)).then_inc(w_hi, 1)
                else:
                    staged(act, c)
                    nc.scalar.mul(hi_of(c), staged_of(c), W_SCALE).then_inc(w_hi, 1)

            def norm1(t):
                act.wait_ge(rstd1, t + 1)
                if t >= 2:
                    act.wait_ge(xln_turned, t - 1)
                nc.scalar.activation(xln[0:T, t % 2], h[0:T, t % RING], ACT.Identity,
                                     scale=rstd[0:T, t % 2:t % 2 + 1],
                                     bias=shift[0:T, t % 2:t % 2 + 1]).then_inc(xln_ready, 1)

            def norm2(t):
                act.wait_ge(rstd2, t + 1)
                if t >= 2:
                    act.wait_ge(row_lo_ready, t - 1)
                at = slice(2 + t % 2, 3 + t % 2)
                for dst in (xln2[0:T, t % 2], rows[0:T, t, 0:D]):
                    last = nc.scalar.activation(dst, h2[0:T, t % 4], ACT.Identity, scale=rstd[0:T, at],
                                                bias=shift[0:T, at])
                last.then_inc(row_hi_ready, 1)

            def exp_gap(t):
                act.wait_ge(gap_ready, t + 1)
                nc.scalar.activation(gate_gap[0:T, 1, t:t + 1], gate_gap[0:T, 0, t:t + 1],
                                     ACT.Exp).then_inc(gap_exp, 1)

            for s in range(STEPS):
                if s == 2:
                    act.wait_ge(attn_in, 7 * 16)
                    nc.scalar.activation(keep[0:T, HEADS:], s_beta[0:T], ACT.Exp,
                                         scale=-1.0).then_inc(beta_exp, 1)
                    nc.scalar.mul(gate_pair[:, :, 0], s_wg, W_SCALE).then_inc(gate_hi, 1)
                if 0 <= s - 3 < NT:
                    copy_prob_t(s - 3)
                if 0 <= s - 1 < NT:
                    copy_xln_t(s - 1)
                if 0 <= s - 4 < NT:
                    copy_attn_t(s - 4)
                if 0 <= s - 2 < NT:
                    exps(s - 2)
                if 0 <= s - 1 < NT:
                    copy_qkv(s - 1)
                    tanh_q(s - 1)
                if 0 <= s - 5 < NT:
                    copy_x2_t(s - 5)
                if s < NT:
                    norm1(s)
                if 0 <= s - 4 < NT:
                    norm2(s - 4)
                if 0 <= s - 5 < NT:
                    exp_gap(s - 5)
                for c in chunks_at(s):
                    split_hi(c)

            def copy_x_t(n, b, m, first=False):
                act.wait_ge(x_turned, n + 1)
                if not first:
                    act.wait_ge(hid_ready, 2 * n - 2)
                v_ = bank[4][:].bitcast(F16)[:, 0:4 * P].rearrange("p (a b) -> p a b", b=P)
                d_ = x_t[:, b].rearrange("p (a b) -> p a b", b=P)
                nc.scalar.copy(d_[:, :, 0:m], v_[:, :, 0:m]).then_inc(x_t_ready, 1)

            def silu(n, b, m, first=False):
                for half_ in range(2):
                    act.wait_ge(hid_ready, 2 * n + half_ + 1)
                    if not first:
                        act.wait_ge(lo_ready, 2 * n + half_ - 1)
                    d_ = act_out[:, half_].rearrange("p (a b) -> p a b", b=P)[:, :, 0:m]
                    s_ = bank[2 * b + half_][:].rearrange("p (a b) -> p a b", b=P)[:, :, 0:m]
                    nc.scalar.activation(d_, s_, ACT.Silu,
                                         scale=1.0 / (X_SCALE * W_SCALE)).then_inc(hid_acted, 1)

            copy_x_t(0, 0, T, first=True)
            silu(0, 0, T, first=True)
            copy_x_t(1, 1, T, first=True)
            act.wait_ge(wo_ready, NT)
            act.wait_ge(logits_ready, NT)
            act.wait_ge(row_lo_ready, NT)
            for q in range(4):
                act.wait_ge(h2_stored[q], 16 * len(range(q, NT, 4)))
            for t in range(1, NT - 1):
                silu(t, t % 2, T)
                copy_x_t(t + 1, (t + 1) % 2, T)
                if t == 7:
                    act.wait_ge(inverse_ready, 1)
                for c in late_at(t):
                    assert t >= 7 or (c + 1) * 2 * CHUNK <= (EXPERTS + 1) * EW - 2 * table_words
                    split_hi(c)
            silu(NT - 1, 0, T)
            copy_x_t(NT, 1, P)
            with act.Fori(0, (SLOT_TILES - 2) // 2) as i:
                for r in range(2):
                    n = 2 * i + r + NT
                    silu(n, (NT + r) % 2, P)
                    copy_x_t(n + 1, (NT + r + 1) % 2, P)
            n = NT + (SLOT_TILES - 2) // 2 * 2
            for n in range(n, NT + SLOT_TILES):
                silu(n, n % 2, P)
                if n + 1 < NT + SLOT_TILES:
                    copy_x_t(n + 1, (n + 1) % 2, P)

        @block.gpsimd
        def _(pool):
            steps_done = [0]

            def link(ins):
                steps_done[0] += 1
                ins.then_inc(pool_step, 1)
                pool.wait_ge(pool_step, steps_done[0])

            def inv_std(t, src, done, slot, scale):
                pool.wait_ge(src, t + 1)
                v_, y_ = var_eps[0:T, slot:slot + 1], rstd[0:T, slot:slot + 1]
                t_ = newton[0:T, slot:slot + 1]
                link(nc.gpsimd.tensor_scalar_add(v_, mv[0:T, slot, 1:2], EPS))
                link(nc.gpsimd.tensor_tensor(y_, v_, half[0:T, 0:1], ALU.pow))
                link(nc.gpsimd.tensor_tensor(t_, y_, y_, ALU.mult))
                link(nc.gpsimd.tensor_tensor(t_, t_, v_, ALU.mult))
                link(nc.gpsimd.tensor_scalar(t_, t_, -0.5 * scale, 1.5 * scale, ALU.mult, ALU.add))
                link(nc.gpsimd.tensor_tensor(y_, y_, t_, ALU.mult))
                nc.gpsimd.tensor_scalar(shift[0:T, slot:slot + 1], y_, mv[0:T, slot, 0:1], -1.0,
                                        ALU.mult, ALU.mult).then_inc(done, 1)

            def q_terms(t):
                pool.wait_ge(q_tanh_ready, t + 1)
                if t >= 1:
                    pool.wait_ge(sq_ready, t)
                nc.gpsimd.tensor_scalar(q_num, q_min[:, t % 2], 1.0, 1.0, ALU.mult, ALU.add)
                nc.gpsimd.tensor_scalar(q_den, q_min[:, t % 2], -1.0, 1.0, ALU.mult,
                                        ALU.add).then_inc(q_terms_ready, 1)

            def scale_weights(c):
                staged(pool, c)
                nc.gpsimd.tensor_scalar(stage[:, c % STAGES], stage[:, c % STAGES], W_SCALE, 1.0,
                                        ALU.mult, ALU.mult).then_inc(w_scaled, 1)

            def split_lo(c):
                pool.wait_ge(w_hi, c + 1)
                nc.gpsimd.tensor_tensor(lo_of(c), staged_of(c), hi_of(c),
                                        ALU.subtract).then_inc(w_lo_pool, 1)

            link(nc.gpsimd.memset(half[:], -0.5))
            nc.gpsimd.memset(y[:, 2], 0.0).then_inc(dummy_zero, 1)
            nc.gpsimd.memset(ones[:], 1.0).then_inc(ones_ready, 1)
            for s in range(STEPS):
                if s < NT:
                    inv_std(s, stats1, rstd1, s % 2, 1.0)
                    if s == 0:
                        pool.wait_ge(consts_in, 5 * 16)
                    pool.wait_ge(h_ready, s + 1)
                    if s >= RING:
                        pool.wait_ge(h2_ready, s - RING + 1)
                    nc.gpsimd.tensor_tensor(h_bo[0:T, s % RING], h[0:T, s % RING], s_ob[0:T],
                                            ALU.add).then_inc(h_bo_ready, 1)
                if 0 <= s - 1 < NT:
                    q_terms(s - 1)
                if 0 <= s - 4 < NT:
                    inv_std(s - 4, stats2, rstd2, 2 + s % 2, X_SCALE)
                for c in filter(by_pool, chunks_at(s)):
                    scale_weights(c)
                for c in filter(by_pool, chunks_at(s)):
                    split_lo(c)

            def gather(j):
                if j >= 4:
                    pool.wait_ge(x_turned, NT + j - 3)
                nc.gpsimd.indirect_dma_start(
                    out=slot_rows[:, j % 4], out_offset=None, in_=x_rows,
                    in_offset=bass.IndirectOffsetOnAxis(ap=gather_id[:, j:j + 1], axis=0)
                ).then_inc(slot_rows_in[j % 4], 16)

            for q in range(4):
                pool.wait_ge(h2_stored[q], 16 * len(range(q, NT, 4)))
            for t in range(NT):
                for c in filter(by_pool, late_at(t + 1)):
                    scale_weights(c)
                if t == 2:
                    pool.wait_ge(tile_hots_ready, 1)
                    for k in range(2):
                        at = slice(k * NT, (k + 1) * NT)
                        for n, value in enumerate((s_tid[0:T], *(gate_parts[0:T, q, k] for q in range(3)))):
                            last = nc.gpsimd.tensor_tensor(
                                in_tile[0:T, at, n], in_tile[0:T, at, 4],
                                value.rearrange("p (a b) -> p a b", b=1).broadcast_to([T, NT, SLOT_TILES]),
                                ALU.mult)
                    last.then_inc(tile_values_ready, 1)
                if t == 7:
                    pool.wait_ge(slots_known, 1)
                    pool.wait_ge(rows_out, 16 * NT)
                    for j in range(4):
                        gather(j)
                m = T if t < NT - 1 else LAST
                pool.wait_ge(y_scaled, t + 1)
                pool.dma_start(out[t * T:t * T + m], y[0:m, t % 3],
                               accum_op=ALU.add).then_inc(shared_out[t % 3], 16)
                for c in filter(by_pool, late_at(t + 1)):
                    split_lo(c)
            for q in range(3):
                pool.wait_ge(shared_out[q], 16 * len(range(q, NT, 3)))

            pool.wait_ge(dummy_out, 16)
            for j in range(SLOT_TILES):
                pool.wait_ge(y_scaled, NT + j + 1)
                if j:
                    pool.wait_ge(added, 16 * j)
                nc.gpsimd.indirect_dma_start(
                    out=out, out_offset=bass.IndirectOffsetOnAxis(ap=add_id[:, j:j + 1], axis=0),
                    in_=y[:, (NT + j) % 2], in_offset=None, compute_op=ALU.add).then_inc(added, 16)
                if j + 4 < SLOT_TILES:
                    gather(j + 4)
            pool.wait_ge(added, 16 * SLOT_TILES)

        @block.vector
        def _(dve):
            steps_done = [0]

            def link(ins):
                steps_done[0] += 1
                ins.then_inc(dve_step, 1)
                dve.wait_ge(dve_step, steps_done[0])

            def max_score(t):
                dve.wait_ge(scores_ready, t + 1)
                for odd in range(2):
                    last = nc.vector.tensor_reduce(
                        neg_max[0:T, t % 2, 2 * odd:2 * odd + 2],
                        bank[7 * odd][0:T, 0:2 * T].rearrange("p (a b) -> p a b", b=T), AX_X, ALU.max,
                        negate=True)
                last.then_inc(max_ready, 1)

            def layer_stats(src, slot, done):
                link(nc.vector.bn_stats(stats[0:T, slot // 2], src))
                nc.vector.bn_aggr(mv[0:T, slot], stats[0:T, slot // 2]).then_inc(done, 1)

            def embed_h(t):
                dve.wait_ge(embed_ready, t + 1)
                nc.vector.tensor_tensor(h[0:T, t % RING], bank[4][0:T, 0:D], s_eb[0:T],
                                        ALU.add).then_inc(h_ready, 1)
                dve.wait_ge(h_ready, t + 1)
                layer_stats(h[0:T, t % RING], t % 2, stats1)

            def min_q(t):
                dve.wait_ge(qk_copied, t + 1)
                nc.vector.tensor_scalar(q_min[:, t % 2], qk_t[:, t % 2, 0:2], 0.0, None,
                                        ALU.min).then_inc(q_min_ready, 1)

            def finish_sq(t):
                dve.wait_ge(q_terms_ready, t + 1)
                link(nc.vector.reciprocal(q_den, q_den))
                link(nc.vector.tensor_tensor(q_den, q_num, q_den, ALU.mult))
                if t >= 3:
                    dve.wait_ge(mixed_ready, t - 2)
                nc.vector.scalar_tensor_tensor(out=sq[:, t % 3], in0=qk_t[:, t % 2, 0:2], scalar=0.0,
                                               in1=q_den, op0=ALU.max, op1=ALU.add).then_inc(sq_ready, 1)

            def heads(ap):
                return ap.rearrange("p (a b) -> p a b", b=HD)

            def per_head(ap):
                return ap.rearrange("p (a b) -> p a b", b=1).broadcast_to([T, HEADS, HD])

            def combine(t):
                dve.wait_ge(prob_ready, t + 1)
                dve.wait_ge(mixed_ready, t + 1)
                both = mix[0:T, t % 4]
                nc.vector.tensor_scalar(both[:, 0:HEADS], bank[1][0:T, 0:HEADS], 1e-6, None,
                                        ALU.add).then_inc(dens_ready, 1)
                dve.wait_ge(dens_ready, t + 1)
                link(nc.vector.reciprocal(both, both))
                link(nc.vector.tensor_tensor(share[0:T], both, keep[0:T], ALU.mult))
                nc.vector.tensor_tensor(heads(read[0:T]), heads(bank[7][0:T, D:2 * D]),
                                        per_head(share[0:T, 0:HEADS]), ALU.mult)
                if t >= 2:
                    dve.wait_ge(attn_turned, t - 1)
                link(nc.vector.tensor_tensor(heads(attn[0:T, t % 2]), heads(bank[7][0:T, 0:D]),
                                             per_head(share[0:T, HEADS:]), ALU.mult))
                nc.vector.tensor_tensor(attn[0:T, t % 2], attn[0:T, t % 2], read[0:T],
                                        ALU.add).then_inc(attn_ready, 1)

            def residual(t):
                dve.wait_ge(wo_ready, t + 1)
                dve.wait_ge(h_bo_ready, t + 1)
                if t >= 4:
                    dve.wait_ge(row_hi_ready, t - 3)
                    dve.wait_ge(h2_stored[t % 4], 16 * (t // 4))
                nc.vector.tensor_tensor(h2[0:T, t % 4], bank[4][0:T, D:2 * D], h_bo[0:T, t % RING],
                                        ALU.add).then_inc(h2_ready, 1)
                dve.wait_ge(h2_ready, t + 1)
                layer_stats(h2[0:T, t % 4], 2 + t % 2, stats2)

            def row_lo(t):
                dve.wait_ge(row_hi_ready, t + 1)
                nc.vector.tensor_tensor(rows[0:T, t, D:2 * D], xln2[0:T, t % 2], rows[0:T, t, 0:D],
                                        ALU.subtract).then_inc(row_lo_ready, 1)

            logit = sb("logit", [P, 8])

            def top2(t):
                dve.wait_ge(logits_ready, t + 1)
                link(nc.vector.tensor_scalar(logit[0:T], bank[6][0:T, D:D + EXPERTS],
                                             1.0 / (X_SCALE * W_SCALE), None, ALU.mult))
                link(nc.vector.max(top[0:T, t], logit[0:T]))
                nc.vector.max_index(top_at[0:T, t], top[0:T, t], logit[0:T]).then_inc(top_done, 1)
                nc.vector.tensor_tensor(gate_gap[0:T, 0, t:t + 1], top[0:T, t, 1:2], top[0:T, t, 0:1],
                                        ALU.subtract).then_inc(gap_ready, 1)

            def split_lo(c):
                dve.wait_ge(w_hi, c + 1)
                nc.vector.scalar_tensor_tensor(out=lo_of(c), in0=staged_of(c), scalar=W_SCALE,
                                               in1=hi_of(c), op0=ALU.mult,
                                               op1=ALU.subtract).then_inc(w_lo_dve, 1)

            dve.wait_ge(consts_in, 5 * 16)
            for s in range(STEPS):
                if s == 3:
                    dve.wait_ge(attn_in, 7 * 16)
                    dve.wait_ge(beta_exp, 1)
                    link(nc.vector.tensor_scalar(keep[0:T, 0:HEADS], keep[0:T, HEADS:], 1.0, None, ALU.add))
                    link(nc.vector.reciprocal(keep[0:T, 0:HEADS], keep[0:T, 0:HEADS]))
                    nc.vector.tensor_scalar(keep[0:T, HEADS:], keep[0:T, 0:HEADS], -1.0, 1.0, ALU.mult,
                                            ALU.add)
                    dve.wait_ge(gate_hi, 1)
                    nc.vector.scalar_tensor_tensor(out=gate_pair[:, :, 1], in0=s_wg, scalar=W_SCALE,
                                                   in1=gate_pair[:, :, 0], op0=ALU.mult,
                                                   op1=ALU.subtract).then_inc(gate_pair_ready, 1)
                if s < NT:
                    embed_h(s)
                if 0 <= s - 2 < NT:
                    max_score(s - 2)
                for c in chunks_at(s - 1):
                    if not by_pool(c):
                        split_lo(c)
                if 0 <= s - 1 < NT:
                    min_q(s - 1)
                if 0 <= s - 4 < NT:
                    residual(s - 4)
                if 0 <= s - 3 < NT:
                    combine(s - 3)
                if 0 <= s - 5 < NT:
                    top2(s - 5)
                if 0 <= s - 1 < NT:
                    finish_sq(s - 1)
                if 0 <= s - 4 < NT:
                    row_lo(s - 4)

            def over(ap, *dims):
                return ap.broadcast_to([T, *dims])

            dve.wait_ge(route_in, 7 * 16)
            dve.wait_ge(top_done, NT)
            link(nc.vector.tensor_copy(top_f[0:T].rearrange("p k t -> p t k"), top_at[0:T, :, 0:2]))
            for k in range(2):
                link(nc.vector.tensor_tensor(
                    pick[0:T, k], over(s_iota[0:T, 0:8].rearrange("p (a b) -> p a b", a=1), NT, 8),
                    over(top_f[0:T, k].rearrange("p (a b) -> p a b", b=1), NT, 8), ALU.is_equal))
            link(nc.vector.tensor_tensor(prod[0:T, 0], pick[0:T, 0], pick[0:T, 1], ALU.add))
            link(nc.vector.memset(member[0:T, NT:NT + 1], 0.0))
            nc.vector.tensor_tensor(member[0:T, 0:NT], prod[0:T, 0],
                                    over(s_valid[0:T].rearrange("p (a b) -> p a b", b=1), NT, 8),
                                    ALU.mult).then_inc(members_ready, 1)

            def find_slots():
                dve.wait_ge(gap_exp, NT)
                link(nc.vector.tensor_scalar(gates[0:T, 1], gate_gap[0:T, 1], 1.0, None, ALU.add))
                link(nc.vector.reciprocal(gates[0:T, 0], gates[0:T, 1]))
                link(nc.vector.tensor_tensor(gates[0:T, 1], gates[0:T, 0], gate_gap[0:T, 1], ALU.mult))
                dve.wait_ge(ranks_ready, 1)
                link(nc.vector.tensor_copy(rank[0:T], bank[7][0:T, 0:(NT + 1) * 8].rearrange(
                    "p (a b) -> p a b", b=8)))
                link(nc.vector.tensor_tensor(
                    tiles_cmp[0:T], over(rank[0:T, NT].rearrange("p (a b) -> p a b", b=1), 8, 10),
                    over(s_steps[0:T].rearrange("p (a b) -> p a b", a=1), 8, 10), ALU.is_gt))
                link(nc.vector.tensor_reduce(tiles_of[0:T, 0], tiles_cmp[0:T], AX_X, ALU.add))
                link(nc.vector.tensor_tensor(
                    tri[0:T], over(tiles_of[0:T, 0].rearrange("p (a b) -> p a b", a=1), 8, 8),
                    s_lower[0:T], ALU.mult))
                link(nc.vector.tensor_reduce(tiles_of[0:T, 1], tri[0:T], AX_X, ALU.add))
                link(nc.vector.tensor_tensor(tiles_of[0:T, 2], tiles_of[0:T, 1], tiles_of[0:T, 0], ALU.add))
                link(nc.vector.tensor_scalar(tiles_of[0:T, 1], tiles_of[0:T, 1], float(P), None, ALU.mult))
                link(nc.vector.tensor_tensor(
                    rank[0:T, 0:NT], rank[0:T, 0:NT],
                    over(tiles_of[0:T, 1].rearrange("p (a b) -> p a b", a=1), NT, 8), ALU.add))
                for k in range(2):
                    link(nc.vector.tensor_tensor(prod[0:T, k], rank[0:T, 0:NT], pick[0:T, k], ALU.mult))
                for k in range(2):
                    link(nc.vector.tensor_reduce(slot_f[0:T, 0, k * NT:(k + 1) * NT], prod[0:T, k], AX_X,
                                                 ALU.add))
                link(nc.vector.tensor_scalar(slot_f[0:T, 1], slot_f[0:T, 0], 1.0 / P, -63.5 / P,
                                             ALU.mult, ALU.add))
                link(nc.vector.tensor_scalar(slot_f[0:T, 1], slot_f[0:T, 1], ROUND, -ROUND, ALU.add,
                                             ALU.add))
                link(nc.vector.scalar_tensor_tensor(out=slot_f[0:T, 2], in0=slot_f[0:T, 1],
                                                    scalar=-float(P), in1=slot_f[0:T, 0], op0=ALU.mult,
                                                    op1=ALU.add))
                for k in range(2):
                    half_ = slot_f[0:T, 1, k * NT:(k + 1) * NT]
                    link(nc.vector.scalar_tensor_tensor(out=half_, in0=half_, scalar=1.0,
                                                        in1=s_valid[0:T], op0=ALU.add, op1=ALU.mult))
                link(nc.vector.tensor_tensor(
                    end_cmp[0:T], over(tiles_of[0:T, 2].rearrange("p (a b) -> p a b", a=1), SLOT_TILES, 8),
                    over(s_iota[0:T, 0:SLOT_TILES].rearrange("p (a b) -> p a b", b=1), SLOT_TILES, 8),
                    ALU.is_le))
                link(nc.vector.tensor_reduce(exp_f[0:T, 0], end_cmp[0:T], AX_X, ALU.add))
                link(nc.vector.tensor_scalar(exp_f[0:T, 1], exp_f[0:T, 0], EXPERTS - 1.0, 1.0, ALU.min,
                                             ALU.add))
                nc.vector.tensor_scalar(expert_of[0:T], exp_f[0:T, 1], float(EW), None,
                                        ALU.mult).then_inc(experts_known, 1)

            def fill_tiles():
                link(nc.vector.tensor_scalar(gate_rest[0:T], gates[0:T], G_SCALE, None, ALU.mult))
                for q in range(3):
                    link(nc.vector.tensor_copy(gate_parts[0:T, q], gate_rest[0:T]))
                    if q < 2:
                        link(nc.vector.tensor_tensor(gate_rest[0:T], gate_rest[0:T], gate_parts[0:T, q],
                                                     ALU.subtract))
                one = in_tile[0:T, :, 4]
                nc.vector.tensor_tensor(
                    one, over(s_iota[0:T, 1:SLOT_TILES + 1].rearrange("p (a b) -> p a b", a=1),
                              2 * NT, SLOT_TILES),
                    over(slot_f[0:T, 1].rearrange("p (a b) -> p a b", b=1), 2 * NT, SLOT_TILES),
                    ALU.is_equal).then_inc(tile_hots_ready, 1)

            def fill_rows(k):
                at = slice(k * NT, (k + 1) * NT)
                last = nc.vector.tensor_tensor(
                    in_row[0:T, at], over(s_iota[0:T].rearrange("p (a b) -> p a b", a=1), NT, P),
                    over(slot_f[0:T, 2, at].rearrange("p (a b) -> p a b", b=1), NT, P), ALU.is_equal)
                if k:
                    last.then_inc(tables_ready, 1)
                else:
                    link(last)

            def slot_tables():
                dve.wait_ge(inverse_ready, 1)
                n = SLOT_TILES
                link(nc.vector.tensor_scalar(vacant[:], bank[7][:, 4 * n:5 * n], -1.0, 1.0, ALU.mult,
                                             ALU.add))
                nc.vector.tensor_copy(gather_id[:], bank[7][:, 0:n])
                nc.vector.scalar_tensor_tensor(out=add_id[:], in0=vacant[:], scalar=s_dummy[:, 0:1],
                                               in1=bank[7][:, 0:n], op0=ALU.mult,
                                               op1=ALU.add).then_inc(slots_known, 1)
                link(nc.vector.tensor_reduce(
                    gate_sum[:], bank[7][:, n:4 * n].rearrange("p (a b) -> p b a", b=n), AX_X, ALU.add))
                link(nc.vector.tensor_scalar(slot_gate[:], gate_sum[:],
                                             1.0 / (G_SCALE * H_SCALE * W_SCALE), None, ALU.mult))

            def split_hidden(n, b, m, first=False):
                for half_ in range(2):
                    dve.wait_ge(hid_acted, 2 * n + half_ + 1)
                    if not first and half_ == 0:
                        dve.wait_ge(y_ready, n - 1)
                    src = act_out[:, half_].rearrange("p (a b) -> p a b", b=P)[:, :, 0:m]

                    def four(ap):
                        return ap[:, b, half_ * 512:half_ * 512 + 512].rearrange(
                            "p (a b) -> p a b", b=P)[:, :, 0:m]

                    nc.vector.tensor_scalar(four(hid_hi), src, H_SCALE, None, ALU.mult).then_inc(hi_ready, 1)
                    dve.wait_ge(hi_ready, 2 * n + half_ + 1)
                    nc.vector.scalar_tensor_tensor(out=four(hid_lo), in0=src, scalar=H_SCALE,
                                                   in1=four(hid_hi), op0=ALU.mult,
                                                   op1=ALU.subtract).then_inc(lo_ready, 1)

            def output(n, b, m, dst, scale):
                dve.wait_ge(y_ready, n + 1)
                nc.vector.tensor_scalar(dst, bank[5 + b][0:m, 0:D], scale, None,
                                        ALU.mult).then_inc(y_half, 1)
                dve.wait_ge(y_half, n + 1)
                nc.vector.scalar_tensor_tensor(out=dst, in0=bank[5 + b][0:m, D:2 * D], scalar=scale,
                                               in1=dst, op0=ALU.mult, op1=ALU.add).then_inc(y_scaled, 1)

            def shared_y(t):
                if t >= 3:
                    dve.wait_ge(shared_out[t % 3], 16 * (t // 3))
                output(t, t % 2, T, y[0:T, t % 3], 1.0 / (H_SCALE * W_SCALE))

            split_hidden(0, 0, T, first=True)
            dve.wait_ge(dummy_out, 16)
            find_slots()
            for t in range(1, NT):
                split_hidden(t, t % 2, T, first=(t == 1))
                shared_y(t - 1)
                if t == 2:
                    fill_tiles()
                if t in (3, 4):
                    fill_rows(t - 3)
                if t == 5:
                    slot_tables()
                for c in late_at(t):
                    if not by_pool(c):
                        split_lo(c)

            def slot_y(j, b):
                output(NT + j, b, P, y[:, b], slot_gate[:, bass.ds(j, 1)])

            split_hidden(NT, NT % 2, P)
            shared_y(NT - 1)
            split_hidden(NT + 1, (NT + 1) % 2, P)
            for q in range(3):
                dve.wait_ge(shared_out[q], 16 * len(range(q, NT, 3)))
            slot_y(0, NT % 2)
            split_hidden(NT + 2, NT % 2, P)
            slot_y(1, (NT + 1) % 2)

            def slot_step(j, r):
                split_hidden(NT + j, (NT + r) % 2, P)
                dve.wait_ge(added, 16 * (j - 2))
                slot_y(j - 1, (NT + r + 1) % 2)

            SLOT_LOOP = (SLOT_TILES - 3) // 4
            with dve.Fori(0, SLOT_LOOP) as i:
                for r in range(3, 7):
                    slot_step(4 * i + r, r % 4)
            for j in range(4 * SLOT_LOOP + 3, SLOT_TILES):
                slot_step(j, j % 4)
            dve.wait_ge(added, 16 * (SLOT_TILES - 2))
            slot_y(SLOT_TILES - 1, (NT + SLOT_TILES - 1) % 2)


def kernel(x, cls_tok, L0_tok_W, L0_tok_b, L0_attn_Wq, L0_attn_Wk, L0_attn_Wv, L0_attn_Wo, L0_attn_bo,
           L0_attn_betas, L0_attn_mem, L0_attn_z, L0_ffn_shared_w1, L0_ffn_shared_w2,
           L0_ffn_experts_w1, L0_ffn_experts_w2, L0_ffn_gate_w):
    import ml_dtypes
    import numpy as np
    import concourse.bacc as bacc
    from concourse.bass_utils import run_bass_kernel_spmd

    f32 = np.float32

    def fold(w):
        k, n = w.shape
        return w.reshape(k // P, P, n).transpose(1, 0, 2).reshape(P, -1)

    px = np.asarray(x).reshape(IMAGES, 3, 6, 16, 6, 16).transpose(0, 2, 4, 1, 3, 5).reshape(IMAGES, 36, PATCH)
    padded = np.zeros((NT * PER_TILE, SEQ, PATCH), f32)
    padded[:IMAGES, 1:] = px
    patches = padded.reshape(NT, T, PC, P).transpose(0, 3, 2, 1).reshape(NT, P, PC * T)

    eb = np.concatenate([np.asarray(cls_tok).reshape(1, D), np.broadcast_to(L0_tok_b, (SEQ - 1, D))])
    embed_bias = np.concatenate([eb] * PER_TILE)
    wq, wk = np.asarray(L0_attn_Wq).T, np.asarray(L0_attn_Wk).T
    w_qk = np.concatenate([wq, wk], axis=1)
    mem = np.zeros((P, KC, P), f32)
    z = np.zeros((P, KC, 2), f32)
    for hd in range(HEADS):
        at = slice(HD * (hd % 2), HD * (hd % 2) + HD)
        mem[at, hd // 2, at] = L0_attn_mem[hd]
        z[at, hd // 2, hd % 2] = np.asarray(L0_attn_z)[hd, :, 0]
    w1 = np.concatenate([np.asarray(L0_ffn_shared_w1)[None], np.asarray(L0_ffn_experts_w1)])
    w2 = np.concatenate([np.asarray(L0_ffn_shared_w2)[None], np.asarray(L0_ffn_experts_w2)])
    n = EXPERTS + 1
    w1 = w1.transpose(0, 2, 1).reshape(n, KC, P, HIDDEN).transpose(0, 2, 1, 3).reshape(n, P, KC * HIDDEN)
    w2 = w2.transpose(0, 2, 1).reshape(n, HC, P, D).transpose(0, 2, 1, 3).reshape(n, P, HC * D)

    tok = np.arange(T)
    same = tok[:, None] // SEQ == tok[None, :] // SEQ
    causal = np.where(same & (tok[None, :] <= tok[:, None]), 0.0, -1e30)
    causal = np.concatenate([causal, causal], axis=1).astype(ml_dtypes.bfloat16)
    dummy_id = (TOKENS + np.arange(P, dtype=f32))[:, None]
    token_id = (np.arange(NT)[None, :] * T + tok[:, None]).astype(f32)
    valid = (token_id < TOKENS).astype(f32)
    steps = (P * np.arange(10)).astype(f32)

    ins = dict(
        patches=patches, w_embed=fold(np.asarray(L0_tok_W).T), embed_bias=embed_bias, w_qk=fold(w_qk),
        w_v=fold(np.asarray(L0_attn_Wv).T), w_o=fold(np.asarray(L0_attn_Wo).T),
        out_bias=np.broadcast_to(L0_attn_bo, (T, D)),
        betas=np.broadcast_to(np.asarray(L0_attn_betas).reshape(1, HEADS), (T, HEADS)),
        mem=mem.reshape(P, -1), z=z.reshape(P, -1), w_ffn=np.concatenate([w1, w2], axis=2),
        w_gate=fold(np.asarray(L0_ffn_gate_w).T),
        ident=np.eye(P, dtype=f32), ident16=np.eye(P, dtype=np.float16), causal=causal,
        before=(tok[:, None] < tok[None, :]).astype(np.float16), valid=valid, token_id=token_id,
        dummy_id=dummy_id,
        lower=np.broadcast_to((np.arange(8)[None, :] < np.arange(8)[:, None]).astype(f32), (T, 8, 8)),
        iota=np.broadcast_to(np.arange(P, dtype=f32), (P, P)), steps=np.broadcast_to(steps, (T, len(steps))))

    nc = bacc.Bacc("TRN2", target_bir_lowering=False, num_devices=1)
    arrays, args = {}, {}
    for name, a in ins.items():
        a = np.ascontiguousarray(a)
        arrays[f"in_{name}"] = a
        args[name] = nc.dram_tensor(f"in_{name}", a.shape, mybir.dt.from_np(a.dtype), kind="ExternalInput").ap()
    out = nc.dram_tensor("out_rows", (TOKENS + P, D), F32, kind="ExternalOutput").ap()
    build(nc, **args, out=out)
    r = run_bass_kernel_spmd(nc, [arrays], core_ids=[0])
    return r.results[0]["out_rows"][:TOKENS].reshape(IMAGES, SEQ, D)
```
